# Optimizing a Trainium2 kernel written in Bass

```python
import numpy as np
import jax
import jax.numpy as jnp

def _softmax(x, axis=-1):
    return jax.nn.softmax(x, axis=axis)

def _gelu(x):
    return jax.nn.gelu(x, approximate=True)

def _silu(x):
    return jax.nn.silu(x)

def _sigmoid(x):
    return jax.nn.sigmoid(x)

def _layernorm(x, axis=-1, eps=1e-05):
    m = jnp.mean(x, axis=axis, keepdims=True)
    v = jnp.var(x, axis=axis, keepdims=True)
    return (x - m) / jnp.sqrt(v + eps)

def _scatter_add(tgt, idx, src, axis=0):
    return tgt.at[idx].add(src)

def _segment_sum(src, seg, n):
    return jax.ops.segment_sum(src, seg, n)
kernel_name = 'mk_vit_tower_d1_tok_img1024_r4_658b71'

def setup_inputs(seed: int=0):
    np.random.seed(seed)
    _w = jnp.asarray

    def _rec_inputs():
        import jax
        import jax.numpy as jnp
        _rk = jax.random.key(seed)
        x = 7.57192e-06 + 1.00007 * jax.random.normal(jax.random.fold_in(_rk, 1), (32, 3, 64, 64), jnp.float32)
        return x
    x = _rec_inputs()

    def _L0_tok_setup():
        import jax, jax.numpy as jnp
        import numpy as np
        IMG = 224
        PATCH = 16
        C_IN = 3
        D = 256
        B = 64
        PATCH_DIM = C_IN * PATCH * PATCH
        key = jax.random.key(seed)
        k1, k2, k3 = jax.random.split(key, 3)
        x = jax.random.normal(k1, (B, C_IN, IMG, IMG), dtype=jnp.float32)
        W = jax.random.normal(k2, (D, PATCH_DIM), dtype=jnp.float32) * (1.0 / np.sqrt(PATCH_DIM))
        b = jax.random.normal(k3, (D,), dtype=jnp.float32) * 0.02
        return {'x': x, 'W': W, 'b': b}
    _L0_tok_all = _L0_tok_setup()
    _L0_tok_in = {k: v for k, v in _L0_tok_all.items() if k in ('W', 'b')}
    del _L0_tok_all

    def _L0_attn_setup():
        import jax, jax.numpy as jnp
        import numpy as np
        EMB, HEADS, HIDDEN = (256, 16, 64)
        BS, N = (2, 512)
        key = jax.random.key(seed)
        ks = jax.random.split(key, 7)
        s_in = 1.0 / np.sqrt(EMB)
        s_u = 1.0 / np.sqrt(HEADS * HIDDEN)
        return {'x': jax.random.normal(ks[0], (BS, N, EMB), dtype=jnp.float32), 'w_q': jax.random.uniform(ks[1], (EMB, HEADS * HIDDEN), jnp.float32, -s_in, s_in), 'w_k': jax.random.uniform(ks[2], (EMB, HEADS * HIDDEN), jnp.float32, -s_in, s_in), 'w_v': jax.random.uniform(ks[3], (EMB, HEADS * HIDDEN), jnp.float32, -s_in, s_in), 'w_u': jax.random.uniform(ks[4], (HEADS * HIDDEN, EMB), jnp.float32, -s_u, s_u), 'b_u': jax.random.uniform(ks[5], (EMB,), jnp.float32, -s_u, s_u)}
    _L0_attn_all = _L0_attn_setup()
    _L0_attn_in = {k: v for k, v in _L0_attn_all.items() if k in ('w_q', 'w_k', 'w_v', 'w_u', 'b_u')}
    del _L0_attn_all

    def _L0_ffn_setup():
        import jax, jax.numpy as jnp
        import numpy as np
        H = 256
        E = 32
        I = 128
        TOP_K = 6
        IS = 256
        NORM_MIN = 1e-12
        B, S = (2, 256)
        key = jax.random.key(seed)
        ks = jax.random.split(key, 8)
        sc = 0.02
        return {'hidden_states': jax.random.normal(ks[0], (B, S, H), jnp.float32), 'router_weight': jax.random.normal(ks[1], (E, H), jnp.float32) * sc, 'e_score_bias': jnp.zeros((E,), jnp.float32), 'gate_up_proj': jax.random.normal(ks[2], (E, 2 * I, H), jnp.float32) * sc, 'down_proj': jax.random.normal(ks[3], (E, H, I), jnp.float32) * sc, 'shared_gate_w': jax.random.normal(ks[4], (IS, H), jnp.float32) * sc, 'shared_up_w': jax.random.normal(ks[5], (IS, H), jnp.float32) * sc, 'shared_down_w': jax.random.normal(ks[6], (H, IS), jnp.float32) * sc}
    _L0_ffn_all = _L0_ffn_setup()
    _L0_ffn_in = {k: v for k, v in _L0_ffn_all.items() if k in ('router_weight', 'e_score_bias', 'gate_up_proj', 'down_proj', 'shared_gate_w', 'shared_up_w', 'shared_down_w')}
    del _L0_ffn_all
    return {'x': x, 'L0_tok_W': _L0_tok_in['W'], 'L0_tok_b': _L0_tok_in['b'], 'L0_attn_w_q': _L0_attn_in['w_q'], 'L0_attn_w_k': _L0_attn_in['w_k'], 'L0_attn_w_v': _L0_attn_in['w_v'], 'L0_attn_w_u': _L0_attn_in['w_u'], 'L0_attn_b_u': _L0_attn_in['b_u'], 'L0_ffn_router_weight': _L0_ffn_in['router_weight'], 'L0_ffn_e_score_bias': _L0_ffn_in['e_score_bias'], 'L0_ffn_gate_up_proj': _L0_ffn_in['gate_up_proj'], 'L0_ffn_down_proj': _L0_ffn_in['down_proj'], 'L0_ffn_shared_gate_w': _L0_ffn_in['shared_gate_w'], 'L0_ffn_shared_up_w': _L0_ffn_in['shared_up_w'], 'L0_ffn_shared_down_w': _L0_ffn_in['shared_down_w']}

def reference(x, L0_tok_W, L0_tok_b, L0_attn_w_q, L0_attn_w_k, L0_attn_w_v, L0_attn_w_u, L0_attn_b_u, L0_ffn_router_weight, L0_ffn_e_score_bias, L0_ffn_gate_up_proj, L0_ffn_down_proj, L0_ffn_shared_gate_w, L0_ffn_shared_up_w, L0_ffn_shared_down_w):
    import jax
    import jax.numpy as jnp

    def _L0_tok_ref(x, W, b):
        import jax, jax.numpy as jnp
        import numpy as np
        IMG = 224
        PATCH = 16
        C_IN = 3
        D = 256
        B = 64
        PATCH_DIM = C_IN * PATCH * PATCH
        Bx, C, H, Wd = x.shape
        p = PATCH
        Hp, Wp = (H // p, Wd // p)
        patches = x.reshape(Bx, C, Hp, p, Wp, p).transpose(0, 2, 3, 1, 4, 5)
        patches = patches.reshape(Bx, -1, PATCH_DIM)
        return jnp.einsum('bnp,dp->bnd', patches, W) + b

    def _L0_attn_ref(x, w_q, w_k, w_v, w_u, b_u):
        import jax, jax.numpy as jnp
        import numpy as np
        EMB, HEADS, HIDDEN = (256, 16, 64)
        BS, N = (2, 512)
        bs, n, emb = x.shape
        h, hd = (HEADS, HIDDEN)
        q = (x @ w_q).reshape(bs, n, h, hd)
        k = (x @ w_k).reshape(bs, n, h, hd)
        v = (x @ w_v).reshape(bs, n, h, hd)
        scale = 1.0 / jnp.sqrt(jnp.asarray(hd, dtype=x.dtype))
        q = q * scale
        k = k * scale
        dot = jnp.einsum('bqhd,bkhd->bhqk', q, k)
        causal = jnp.tril(jnp.ones((n, n), dtype=bool))
        dot = jnp.where(causal, dot, jnp.asarray(-jnp.inf, dtype=dot.dtype))
        att = jax.nn.softmax(dot, axis=-1)
        out = jnp.einsum('bhqk,bkhd->bqhd', att, v).reshape(bs, n, h * hd)
        return out @ w_u + b_u

    def _L0_ffn_ref(hidden_states, router_weight, e_score_bias, gate_up_proj, down_proj, shared_gate_w, shared_up_w, shared_down_w):
        import jax, jax.numpy as jnp
        import numpy as np
        H = 256
        E = 32
        I = 128
        TOP_K = 6
        IS = 256
        NORM_MIN = 1e-12
        B, S = (2, 256)
        b, s, h = hidden_states.shape
        x = hidden_states.reshape(-1, h)
        T = x.shape[0]
        shared_out = jax.nn.silu(x @ shared_gate_w.T) * (x @ shared_up_w.T) @ shared_down_w.T
        xf = x.astype(jnp.float32)
        router_logits = xf @ router_weight.T
        routing_weights = jax.nn.softmax(router_logits, axis=-1)
        corrected = routing_weights + e_score_bias
        _, top_idx = jax.lax.top_k(corrected, TOP_K)
        top_w = jnp.take_along_axis(routing_weights, top_idx, axis=-1)
        top_w = top_w / jnp.clip(top_w.sum(axis=-1, keepdims=True), NORM_MIN)
        top_w = top_w.astype(x.dtype)
        combine = jnp.zeros((T, E), x.dtype).at[jnp.arange(T)[:, None], top_idx].add(top_w)
        gu = jnp.einsum('th,eih->tei', x, gate_up_proj)
        gate, up = jnp.split(gu, 2, axis=-1)
        hmid = jax.nn.silu(gate) * up
        y = jnp.einsum('tei,ehi->teh', hmid, down_proj)
        out = jnp.einsum('teh,te->th', y, combine) + shared_out
        return out.reshape(b, s, h)
    h = _L0_tok_ref(x, L0_tok_W, L0_tok_b)
    h = h + _L0_attn_ref(_layernorm(h, axis=-1), L0_attn_w_q, L0_attn_w_k, L0_attn_w_v, L0_attn_w_u, L0_attn_b_u)
    h = h + _L0_ffn_ref(_layernorm(h, axis=-1), L0_ffn_router_weight, L0_ffn_e_score_bias, L0_ffn_gate_up_proj, L0_ffn_down_proj, L0_ffn_shared_gate_w, L0_ffn_shared_up_w, L0_ffn_shared_down_w)
    return h

_drawn_inputs = setup_inputs


def setup_inputs(seed=0):
    import zlib

    import numpy as np

    out = dict(_drawn_inputs(seed))
    spreads = {'L0_ffn_e_score_bias': (0.0, 0.8)}
    factors = {'L0_attn_w_q': 8.0,
     'L0_attn_w_k': 8.0,
     'L0_attn_b_u': 3.118,
     'L0_ffn_router_weight': 8.0,
     'L0_ffn_gate_up_proj': 8.0,
     'L0_ffn_down_proj': 8.0,
     'L0_ffn_shared_gate_w': 3.419,
     'L0_ffn_shared_up_w': 3.426,
     'L0_ffn_shared_down_w': 3.409}
    for name, (base, spread) in spreads.items():
        noise = np.random.default_rng([zlib.crc32(name.encode()), seed]).standard_normal(out[name].shape)
        drawn = base * np.exp(spread * noise) if base else spread * noise
        out[name] = jnp.asarray(drawn.astype(out[name].dtype))
    for name, factor in factors.items():
        out[name] = (out[name] * factor).astype(out[name].dtype)
    return out
```

```python
from contextlib import ExitStack

import concourse.bass as bass
from concourse import mybir

P = 128
F32 = mybir.dt.float32
F32R = mybir.dt.float32r
I32 = mybir.dt.int32
U32 = mybir.dt.uint32
ALU = mybir.AluOpType
ACT = mybir.ActivationFunctionType
AX_X = mybir.AxisListType.X

BANK = 512
BLOCK = 32
SEQ = 16
HEAD = 64
TOP_K = 6
LN_EPS = 1e-5
NORM_MIN = 1e-12
MASKED = -3.0e38
MASK_COPIES = 8
LIST = 36
CTL_N = 40
C_IDENT = 0
C_MASK = C_IDENT + P
C_IOTA = C_MASK + MASK_COPIES * BLOCK
C_BEFORE = C_IOTA + TOP_K * 32
C_SLOT = C_BEFORE + 32
C_NUMBER = C_SLOT + LIST
C_ONE = C_NUMBER + 1
C_COLS = C_ONE + 1


def vit_block(nc, xp_d, w_tok_d, b_tok_d, wq_d, wk_d, wv_d, wu_d, bu_d, router_d, ebias_d, experts_d,
              consts_d, out_d):
    KP = xp_d.shape[0]
    T = xp_d.shape[2]
    NT = T // P
    D = w_tok_d.shape[2]
    KD = D // P
    DA = wq_d.shape[2]
    NG = DA // P
    NITEM = experts_d.shape[0]
    E = router_d.shape[2]
    SHARED = NITEM - E
    GU = KD * 2 * P
    ITEM = GU + D
    RAW = 4
    SCORE_SCALE = 1.0 / HEAD

    comb_d = nc.dram_tensor("combine_rows", [E, T], F32, kind="Internal").ap()

    with ExitStack() as ctx:
        def sb(name, shape, dt=F32):
            return ctx.enter_context(nc.sbuf_tensor(name, shape, dt))

        def sem(name):
            return ctx.enter_context(nc.semaphore(name))

        ps = [ctx.enter_context(nc.psum_tensor(f"bank{i}", [P, BANK], F32)) for i in range(2)]
        score_ps = [ctx.enter_context(nc.psum_tensor(f"score_ps{i}", [P, 2 * BANK], F32)) for i in range(2)]
        ps += [ctx.enter_context(nc.psum_tensor(f"bank{i}", [P, BANK], F32)) for i in range(6, 8)]
        banks = {0: score_ps[0][:, 0:BANK], 1: score_ps[0][:, BANK:2 * BANK],
                 2: score_ps[1][:, 0:BANK], 3: score_ps[1][:, BANK:2 * BANK],
                 4: ps[0][:, :], 5: ps[1][:, :], 6: ps[2][:, :], 7: ps[3][:, :]}

        consts = sb("consts", [P, C_COLS])
        ident = consts[:, C_IDENT:C_IDENT + P]
        mask8 = consts[:, C_MASK:C_MASK + MASK_COPIES * BLOCK].rearrange("p (a c) -> p a c", c=BLOCK)
        iota6 = consts[:, C_IOTA:C_IOTA + TOP_K * E]
        before = consts[0:E, C_BEFORE:C_BEFORE + E]
        slots = consts[0:E, C_SLOT:C_SLOT + LIST]
        number = consts[0:E, C_NUMBER:C_NUMBER + 1]
        one_col = consts[:, C_ONE:C_ONE + 1]
        b_tok = sb("b_tok", [P, D])
        b_u = sb("b_u", [P, D])
        e_bias = sb("e_bias", [P, E])

        xp = sb("xp", [P, KP * T])
        raw = xp[:, 0:RAW * ITEM].rearrange("p (r n) -> p r n", r=RAW)
        w_tok = sb("w_tok", [P, KP, D])
        stage = sb("stage", [P, 3 * KD * DA])
        stage3 = stage[:, :].rearrange("p (w k n) -> p w k n", w=3, k=KD)
        wu_raw = stage[:, 0:KD * DA].rearrange("p (g n) -> p g n", g=NG)
        tail = KD * DA
        comb_bc = stage[:, tail:tail + RAW * T].rearrange("p (r n) -> p r n", r=RAW)
        gate_act = stage[:, tail + RAW * T:tail + (RAW + 2) * T].rearrange("p (r n) -> p r n", r=2)
        h_mid = stage[:, tail + (RAW + 2) * T:tail + (RAW + 4) * T].rearrange("p (r n) -> p r n", r=2)
        w_hi = sb("w_hi", [P, 3 * KD * DA], F32R)
        w_lo = sb("w_lo", [P, 3 * KD * DA], F32R)
        w_hi3 = w_hi[:, :].rearrange("p (w k n) -> p w k n", w=3, k=KD)
        w_lo3 = w_lo[:, :].rearrange("p (w k n) -> p w k n", w=3, k=KD)
        ex_hi = w_hi[:, 0:2 * ITEM].rearrange("p (r n) -> p r n", r=2)
        ex_lo = w_lo[:, 0:2 * ITEM].rearrange("p (r n) -> p r n", r=2)
        hm_hi = w_hi[:, tail:tail + 2 * T].rearrange("p (r n) -> p r n", r=2)
        hm_lo = w_lo[:, tail:tail + 2 * T].rearrange("p (r n) -> p r n", r=2)
        wu_hi = sb("wu_hi", [P, NG, D], F32R)
        wu_lo = sb("wu_lo", [P, NG, D], F32R)
        rt_raw = sb("rt_raw", [P, KD, E])
        rt_hi = sb("rt_hi", [P, KD, E], F32R)
        rt_lo = sb("rt_lo", [P, KD, E], F32R)

        h = sb("h", [P, NT, D])
        xn = sb("xn", [P, NT, D])
        xt_hi = sb("xt_hi", [P, KD, T], F32R)
        xt_lo = sb("xt_lo", [P, KD, T], F32R)
        stats = sb("stats", [P, NT, 6])
        mv = sb("mv", [P, NT, 2])
        rvar = sb("rvar", [P, NT])
        rstd = sb("rstd", [P, NT])
        q_t = sb("q_t", [P, 2, T])
        k_t = sb("k_t", [P, 2, T])
        v_sb = sb("v_sb", [P, NT, DA])
        A8 = MASK_COPIES
        sc = sb("sc", [P, A8, BLOCK])
        pr = sb("pr", [P, 2, A8, BLOCK])
        mx = sb("mx", [P, A8])
        sm = sb("sm", [P, A8])
        ri = sb("ri", [P, A8])
        pn = sb("pn", [P, A8, BLOCK])
        p_t = sb("p_t", [P, 2, A8, P])
        o_hi = sb("o_hi", [P, NG, T], F32R)
        o_lo = sb("o_lo", [P, NG, T], F32R)
        rl = sb("rl", [P, NT, E])
        re_ = sb("re", [P, NT, E])
        rw = sb("rw", [P, NT, E])
        corr = sb("corr", [P, NT, E])
        top8 = sb("top8", [P, NT, 8])
        idx8 = sb("idx8", [P, NT, 8], U32)
        idxf = sb("idxf", [P, NT, 8])
        hit = sb("hit", [P, NT, TOP_K, E])
        chosen = sb("chosen", [P, NT, E])
        picked = sb("picked", [P, NT, E])
        comb = sb("comb", [P, NT, E])
        r4 = sb("r4", [P, 6, NT])
        comb_t = sb("comb_t", [E, T])
        active = sb("active", [E, 1])
        pos = sb("pos", [E, 1])
        place = sb("place", [E, LIST])
        ctl = sb("ctl", [1, CTL_N + 1], I32)
        h2_t = v_sb[:, 0, 0:KD * T].rearrange("p (k n) -> p k n", k=KD)
        o_sb = v_sb[:, 1, 0:KD * T].rearrange("p (k n) -> p k n", k=KD)

        tok_in = [sem(f"tok_in{c}") for c in range(KP)]
        const_in = sem("const_in")
        bias_in = sem("bias_in")
        small_in = sem("small_in")
        w_in = [sem(f"w_in{i}") for i in range(3)]
        wu_in = sem("wu_in")
        raw_in = [sem(f"raw_in{i}") for i in range(RAW)]
        cb_in = [sem(f"cb_in{i}") for i in range(RAW)]
        comb_out = sem("comb_out")
        tok_mm = sem("tok_mm")
        h_ready = sem("h_ready")
        rvar_ok = sem("rvar_ok")
        rstd_ok = sem("rstd_ok")
        xn_ready = sem("xn_ready")
        xt_ps = sem("xt_ps")
        xt_hi_ok = sem("xt_hi_ok")
        xt_lo_ok = sem("xt_lo_ok")
        w_hi_ok = sem("w_hi_ok")
        w_lo_ok = sem("w_lo_ok")
        wu_hi_ok = sem("wu_hi_ok")
        wu_lo_ok = sem("wu_lo_ok")
        rt_hi_ok = sem("rt_hi_ok")
        rt_lo_ok = sem("rt_lo_ok")
        v_mm = sem("v_mm")
        v_ok_a = sem("v_ok_a")
        v_ok_v = sem("v_ok_v")
        q_mm = sem("q_mm")
        k_mm = sem("k_mm")
        q_ok = sem("q_ok")
        k_ok = sem("k_ok")
        sc_mm = sem("sc_mm")
        sc_out = sem("sc_out")
        sc_sub = sem("sc_sub")
        pr_ok = sem("pr_ok")
        pt_zero = sem("pt_zero")
        pt_ok = sem("pt_ok")
        pv_mm = sem("pv_mm")
        o_hi_ok = sem("o_hi_ok")
        o_lo_ok = sem("o_lo_ok")
        hb_ok = sem("hb_ok")
        u_mm = sem("u_mm")
        step = sem("step")
        rt_mm = sem("rt_mm")
        rt_sub = sem("rt_sub")
        rt_exp = sem("rt_exp")
        comb_ok = sem("comb_ok")
        ct_mm = sem("ct_mm")
        cnt_mm = sem("cnt_mm")
        ct_ok = sem("ct_ok")
        act_ok = sem("act_ok")
        pos_mm = sem("pos_mm")
        place_ok = sem("place_ok")
        list_mm = sem("list_mm")
        ctl_ok = sem("ctl_ok")
        h2_ps = sem("h2_ps")
        h2_ok = sem("h2_ok")
        gu_hi_ok = sem("gu_hi_ok")
        gu_lo_ok = sem("gu_lo_ok")
        dn_hi_ok = sem("dn_hi_ok")
        dn_lo_ok = sem("dn_lo_ok")
        gate_mm = sem("gate_mm")
        up_mm = sem("up_mm")
        silu_ok = sem("silu_ok")
        gc_ok = sem("gc_ok")
        hm_ok = sem("hm_ok")
        hm_hi_ok = sem("hm_hi_ok")
        hm_lo_ok = sem("hm_lo_ok")
        down_mm = sem("down_mm")
        out_ok = sem("out_ok")
        stored = sem("stored")

        def gate_bank(j):
            return banks[0 if j % 2 == 0 else 6]

        def up_bank(j):
            return banks[1 if j % 2 == 0 else 7]

        U_BANK = [6, 7, 0, 1]
        X1_BANK = [4, 5, 6, 7]
        X2_BANK = [2, 3, 4, 5]
        PEEL = 4
        assert SHARED + TOP_K >= PEEL and PEEL == RAW

        block = ctx.enter_context(nc.Block())

        @block.sync
        def _(sp):
            for c in range(KP):
                sp.dma_start(xp[:, c * T:(c + 1) * T], xp_d[c]).then_inc(tok_in[c], 16)
                sp.dma_start(w_tok[:, c, :], w_tok_d[c]).then_inc(tok_in[c], 16)
            sp.dma_start(b_tok[:, :], b_tok_d.broadcast_to([P, D])).then_inc(bias_in, 16)
            sp.dma_start(consts[:, :], consts_d).then_inc(const_in, 16)
            for i, w in enumerate((wv_d, wq_d, wk_d)):
                sp.dma_start(stage3[:, i], w.rearrange("k p n -> p k n")).then_inc(w_in[i], 16)
            sp.dma_start(b_u[:, :], bu_d.broadcast_to([P, D])).then_inc(small_in, 16)
            sp.dma_start(e_bias[:, :], ebias_d.broadcast_to([P, E])).then_inc(small_in, 16)
            sp.dma_start(rt_raw[:, :, :], router_d.rearrange("k p n -> p k n")).then_inc(small_in, 16)
            sp.wait_ge(w_lo_ok, 1)
            sp.dma_start(wu_raw, wu_d.rearrange("g p n -> p g n")).then_inc(wu_in, 16)
            sp.wait_ge(tok_mm, NT)
            for j in range(SHARED):
                sp.dma_start(raw[:, j, :], experts_d[E + j]).then_inc(raw_in[j], 16)
            sp.wait_ge(ct_ok, 1)
            sp.dma_start(comb_d, comb_t[:, :]).then_inc(comb_out, 16)
            sp.wait_ge(ctl_ok, 1)
            n = sp.value_load(ctl[0:1, CTL_N:CTL_N + 1], min_val=TOP_K, max_val=E)

            def load_item(j, b):
                e = sp.value_load(ctl[0:1, bass.ds(j - SHARED, 1)], min_val=0, max_val=E - 1)
                sp.dma_start(raw[:, b, :], experts_d[bass.ds(e, 1)].rearrange("e p n -> (e p) n")
                             ).then_inc(raw_in[b], 16)
                sp.dma_start(comb_bc[:, b, :], comb_d[bass.ds(e, 1), :].broadcast_to([P, T])
                             ).then_inc(cb_in[b], 16)

            sp.wait_ge(comb_out, 16)
            for j in range(SHARED, PEEL):
                load_item(j, j)
            with sp.Fori(PEEL, PEEL + E, RAW) as i:
                for b in range(RAW):
                    with sp.If(n > i + (b - SHARED - 1)):
                        sp.wait_ge(gu_lo_ok, i + (b - RAW + 1))
                        sp.wait_ge(dn_lo_ok, i + (b - RAW + 1))
                        sp.wait_ge(hm_ok, i + (b - RAW + 1))
                        load_item(i + b, b)
            for m in range(KD):
                sp.wait_ge(out_ok, m + 1)
                sp.dma_start(out_d[m], o_sb[:, m, :]).then_inc(stored, 16)
            sp.wait_ge(stored, 16 * KD)

        @block.tensor
        def _(pe):
            for c in range(KP):
                pe.wait_ge(tok_in[c], 32)
                for t in range(NT):
                    mm = pe.matmul(banks[t][:, 0:D], xp[:, c * T + t * P:c * T + (t + 1) * P],
                                   w_tok[:, c, :], start=(c == 0), stop=(c == KP - 1))
                    if c == KP - 1:
                        mm.then_inc(tok_mm, 1)

            def transpose_tiles(nth, bank_of):
                for t in range(NT):
                    pe.wait_ge(xn_ready, nth * NT + t + 1)
                    for k in range(KD):
                        mm = pe.transpose(banks[bank_of[t]][:, k * P:(k + 1) * P],
                                          xn[:, t, k * P:(k + 1) * P], ident)
                    mm.then_inc(xt_ps, 1)

            pe.wait_ge(const_in, 16)
            transpose_tiles(0, X1_BANK)

            pe.wait_ge(w_hi_ok, 1)
            pe.wait_ge(w_lo_ok, 1)
            for t in range(NT):
                pe.wait_ge(xt_hi_ok, t + 1)
                pe.wait_ge(xt_lo_ok, t + 1)
                for half in range(2):
                    n_v = 2 * t + half
                    if n_v >= 4:
                        pe.wait_ge(v_ok_a if half == 0 else v_ok_v, (n_v - 4) // 2 + 1)
                    cols = slice(half * BANK, (half + 1) * BANK)
                    for i in range(3 * KD):
                        k, p = i // 3, i % 3
                        xs = (xt_hi, xt_hi, xt_lo)[p][:, k, t * P:(t + 1) * P]
                        ws = (w_hi3, w_lo3, w_hi3)[p][:, 0, k, cols]
                        mm = pe.matmul(banks[n_v % 4], xs, ws, start=(i == 0), stop=(i == 3 * KD - 1))
                    mm.then_inc(v_mm, 1)

            def project(g, which, bank, done):
                cols = slice(g * P, (g + 1) * P)
                for i in range(3 * KD):
                    k, p = i // 3, i % 3
                    ws = (w_hi3, w_hi3, w_lo3)[p][:, which, k, cols]
                    xs = (xt_hi, xt_lo, xt_hi)[p][:, k, :]
                    mm = pe.matmul(banks[bank], ws, xs, start=(i == 0), stop=(i == 3 * KD - 1))
                mm.then_inc(done, 1)

            def scores(g):
                pe.wait_ge(q_ok, g + 1)
                pe.wait_ge(k_ok, g + 1)
                if g < 2:
                    pe.wait_ge(v_ok_a, NT)
                    pe.wait_ge(v_ok_v, NT)
                else:
                    pe.wait_ge(sc_out, g - 1)
                for a in range(2):
                    rows = slice(HEAD * a, HEAD * (a + 1))
                    for t in range(NT):
                        mm = pe.matmul(score_ps[g % 2][:, (a * NT + t) * P:(a * NT + t + 1) * P],
                                       q_t[rows, g % 2, t * P:(t + 1) * P],
                                       k_t[rows, g % 2, t * P:(t + 1) * P], start=True, stop=True)
                mm.then_inc(sc_mm, 1)

            def values(g):
                pe.wait_ge(pt_ok, g + 1)
                if g < 2:
                    pe.wait_ge(xt_lo_ok, NT)
                else:
                    pe.wait_ge(o_lo_ok, g - 1)
                for a in range(2):
                    for t in range(NT):
                        mm = pe.matmul(banks[4 + g % 2][HEAD * a:HEAD * (a + 1), t * P:(t + 1) * P],
                                       v_sb[:, t, (2 * g + a) * HEAD:(2 * g + a + 1) * HEAD],
                                       p_t[:, g % 2, a * NT + t, :], start=True, stop=True)
                mm.then_inc(pv_mm, 1)

            def output(g):
                pe.wait_ge(o_hi_ok, g + 1)
                pe.wait_ge(o_lo_ok, g + 1)
                pe.wait_ge(wu_hi_ok, g + 1)
                pe.wait_ge(wu_lo_ok, g + 1)
                for t in range(NT):
                    for p in range(3):
                        os_ = (o_hi, o_hi, o_lo)[p][:, g, t * P:(t + 1) * P]
                        ws = (wu_hi, wu_lo, wu_hi)[p][:, g, :]
                        mm = pe.matmul(banks[U_BANK[t]][:, 0:D], os_, ws, start=(g == 0 and p == 0),
                                       stop=(g == NG - 1 and p == 2))
                    if g == NG - 1:
                        mm.then_inc(u_mm, 1)

            pe.wait_ge(w_hi_ok, 3)
            pe.wait_ge(w_lo_ok, 3)
            pe.wait_ge(xt_hi_ok, NT)
            pe.wait_ge(xt_lo_ok, NT)
            for s in range(NG + 2):
                if s < NG:
                    if s >= 1:
                        pe.wait_ge(q_ok, s)
                    project(s, 1, 6, q_mm)
                    if s >= 1:
                        pe.wait_ge(k_ok, s)
                    project(s, 2, 7, k_mm)
                if 1 <= s <= NG:
                    scores(s - 1)
                if s == NG + 1:
                    pe.wait_ge(q_ok, NG)
                    pe.wait_ge(k_ok, NG)
                    pe.wait_ge(sc_out, NG - 1)
                    for g in range(NG - 2):
                        output(g)
                if s >= 2:
                    values(s - 2)
            for g in range(NG - 2, NG):
                output(g)

            pe.wait_ge(sc_out, NG)
            pe.wait_ge(o_lo_ok, NG)
            transpose_tiles(1, X2_BANK)

            pe.wait_ge(rt_hi_ok, 1)
            pe.wait_ge(rt_lo_ok, 1)
            for t in range(NT):
                pe.wait_ge(xt_hi_ok, NT + t + 1)
                pe.wait_ge(xt_lo_ok, NT + t + 1)
                for i in range(3 * KD):
                    k, p = i // 3, i % 3
                    mm = pe.matmul(banks[2][:, t * E:(t + 1) * E],
                                   (xt_hi, xt_hi, xt_lo)[p][:, k, t * P:(t + 1) * P],
                                   (rt_hi, rt_lo, rt_hi)[p][:, k, :], start=(i == 0), stop=(i == 3 * KD - 1))
            mm.then_inc(rt_mm, 1)

            def gate_up(j, b):
                pe.wait_ge(gu_hi_ok, j + 1)
                pe.wait_ge(gu_lo_ok, j + 1)
                for half, bank, done in ((0, gate_bank(b), gate_mm), (1, up_bank(b), up_mm)):
                    if half == 0 and not (type(j) is int and j < 2):
                        pe.wait_ge(silu_ok, j - 1)
                    if half == 1 and not (type(j) is int and j < 2):
                        pe.wait_ge(hm_ok, j - 1)
                    for i in range(3 * KD):
                        k, p = i // 3, i % 3
                        at = k * 2 * P + half * P
                        ws = (ex_hi, ex_hi, ex_lo)[p][:, b % 2, at:at + P]
                        xs = (xt_hi, xt_lo, xt_hi)[p][:, k, :]
                        mm = pe.matmul(bank, ws, xs, start=(i == 0), stop=(i == 3 * KD - 1))
                    mm.then_inc(done, 1)

            def down(j, b, first=False):
                pe.wait_ge(dn_hi_ok, j + 1)
                pe.wait_ge(dn_lo_ok, j + 1)
                pe.wait_ge(hm_hi_ok, j + 1)
                for p in range(3):
                    if p == 2:
                        pe.wait_ge(hm_lo_ok, j + 1)
                    for m in range(KD):
                        ws = (ex_hi, ex_lo, ex_hi)[p][:, b % 2, GU + m * P:GU + (m + 1) * P]
                        hs = (hm_hi, hm_hi, hm_lo)[p][:, b % 2, :]
                        mm = pe.matmul(banks[4 + m], ws, hs, start=(first and p == 0), stop=(p == 2),
                                       skip_group_check=True)
                mm.then_inc(down_mm, 1)

            gate_up(0, 0)
            gate_up(1, 1)
            pe.wait_ge(comb_ok, 1)
            for t in range(NT):
                mm = pe.transpose(banks[3][0:E, t * P:(t + 1) * P], comb[:, t, :], ident)
            mm.then_inc(ct_mm, 1)
            for t in range(NT):
                mm = pe.matmul(banks[2][0:E, 0:1], chosen[:, t, :], one_col, start=(t == 0), stop=(t == NT - 1))
            mm.then_inc(cnt_mm, 1)
            down(0, 0, first=True)
            pe.wait_ge(act_ok, 1)
            pe.matmul(banks[2][0:E, 1:2], before, active[:, :], start=True, stop=True).then_inc(pos_mm, 1)
            pe.wait_ge(place_ok, 1)
            pe.matmul(banks[2][0:1, 0:LIST], number, place[:, :], start=True, stop=True)
            pe.matmul(banks[2][0:1, CTL_N:CTL_N + 1], active[:, :], one_col[0:E, :], start=True,
                      stop=True).then_inc(list_mm, 1)
            down(1, 1)
            pe.wait_ge(ctl_ok, 1)
            pe.wait_ge(ct_ok, 1)
            for k in range(KD):
                for t in range(NT):
                    mm = pe.transpose(banks[2 + k][:, t * P:(t + 1) * P], h[:, t, k * P:(k + 1) * P], ident)
            mm.then_inc(h2_ps, 1)
            n = pe.value_load(ctl[0:1, CTL_N:CTL_N + 1], min_val=TOP_K, max_val=E)
            for j in range(SHARED, PEEL):
                gate_up(j, j)
                if j > SHARED:
                    down(j - 1, j - 1)
            with pe.Fori(PEEL, PEEL + E, RAW) as i:
                for b in range(RAW):
                    with pe.If(n > i + (b - SHARED)):
                        gate_up(i + b, b)
                    with pe.If(n > i + (b - SHARED - 1)):
                        down(i + (b - 1), (b - 1) % RAW)

        @block.scalar
        def _(act):
            def split_hi(dst, src, done):
                nc.scalar.activation(dst, src, ACT.Copy).then_inc(done, 1)

            for i in range(1):
                act.wait_ge(w_in[i], 16)
                split_hi(w_hi3[:, i], stage3[:, i], w_hi_ok)

            def root(nth):
                act.wait_ge(rvar_ok, nth + 1)
                nc.scalar.activation(rstd[:, :], rvar[:, :], ACT.Sqrt).then_inc(rstd_ok, 1)

            def xt_high(nth, bank_of):
                for t in range(NT):
                    act.wait_ge(xt_ps, nth * NT + t + 1)
                    src = banks[bank_of[t]][:, 0:D].rearrange("p (k n) -> p k n", k=KD)
                    split_hi(xt_hi[:, :, t * P:(t + 1) * P], src, xt_hi_ok)

            root(0)
            xt_high(0, X1_BANK)
            for i in range(1, 3):
                act.wait_ge(w_in[i], 16)
                split_hi(w_hi3[:, i], stage3[:, i], w_hi_ok)
            for t in range(NT):
                act.wait_ge(v_mm, 2 * t + 1)
                nc.scalar.activation(v_sb[:, t, 0:BANK], banks[(2 * t) % 4], ACT.Copy).then_inc(v_ok_a, 1)
            act.wait_ge(small_in, 48)
            split_hi(rt_hi[:, :, :], rt_raw[:, :, :], rt_hi_ok)

            def o_high(g):
                act.wait_ge(pv_mm, g + 1)
                split_hi(o_hi[:, g, :], banks[4 + g % 2], o_hi_ok)

            for s in range(NG + 2):
                if s < NG:
                    if s >= 2:
                        act.wait_ge(sc_mm, s - 1)
                    act.wait_ge(q_mm, s + 1)
                    nc.scalar.activation(q_t[:, s % 2, :], banks[6], ACT.Copy).then_inc(q_ok, 1)
                    act.wait_ge(k_mm, s + 1)
                    nc.scalar.activation(k_t[:, s % 2, :], banks[7], ACT.Copy).then_inc(k_ok, 1)
                if 1 <= s <= NG:
                    g = s - 1
                    if g == 0:
                        act.wait_ge(wu_in, 16)
                    split_hi(wu_hi[:, g, :], wu_raw[:, g, :], wu_hi_ok)
                    act.wait_ge(sc_sub, g + 1)
                    nc.scalar.activation(pr[:, g % 2], sc[:, :, :], ACT.Exp).then_inc(pr_ok, 1)
                if s >= 2:
                    o_high(s - 2)

            def gate_up_high(j, b):
                act.wait_ge(raw_in[b], 4 * (j - b) + 16)
                if not (type(j) is int and j < 2):
                    act.wait_ge(up_mm, j - 1)
                split_hi(ex_hi[:, b % 2, 0:GU], raw[:, b, 0:GU], gu_hi_ok)

            def down_high(j, b):
                if not (type(j) is int and j < 2):
                    act.wait_ge(down_mm, j - 1)
                split_hi(ex_hi[:, b % 2, GU:ITEM], raw[:, b, GU:ITEM], dn_hi_ok)

            def silu(j, b):
                act.wait_ge(gate_mm, j + 1)
                if not (type(j) is int and j < 2):
                    act.wait_ge(hm_ok, j - 1)
                nc.scalar.activation(gate_act[:, b % 2, :], gate_bank(b), ACT.Silu).then_inc(silu_ok, 1)

            def h_high(j, b):
                act.wait_ge(hm_ok, j + 1)
                if not (type(j) is int and j < 2):
                    act.wait_ge(down_mm, j - 1)
                split_hi(hm_hi[:, b % 2, :], h_mid[:, b % 2, :], hm_hi_ok)

            act.wait_ge(v_mm, 2 * NT)
            gate_up_high(0, 0)
            down_high(0, 0)
            root(1)
            xt_high(1, X2_BANK)
            gate_up_high(1, 1)
            down_high(1, 1)
            act.wait_ge(rt_sub, 1)
            nc.scalar.activation(re_[:, :, :], rl[:, :, :], ACT.Exp).then_inc(rt_exp, 1)
            silu(0, 0)
            h_high(0, 0)
            silu(1, 1)
            h_high(1, 1)
            act.wait_ge(ctl_ok, 1)
            n = act.value_load(ctl[0:1, CTL_N:CTL_N + 1], min_val=TOP_K, max_val=E)
            gate_up_high(2, 2)
            down_high(2, 2)
            gate_up_high(3, 3)
            silu(2, 2)
            h_high(2, 2)
            down_high(3, 3)
            with act.Fori(PEEL, PEEL + E, RAW) as i:
                for b in range(RAW):
                    with act.If(n > i + (b - SHARED - 1)):
                        gate_up_high(i + b, b)
                        silu(i + (b - 1), (b - 1) % RAW)
                        h_high(i + (b - 1), (b - 1) % RAW)
                        down_high(i + b, b)

        @block.gpsimd
        def _(pool):
            pool.memset(p_t[:, :, :, :], 0.0).then_inc(pt_zero, 1)

            def split_lo(dst, src, hi, done):
                pool.tensor_tensor(dst, src, hi.bitcast(F32), ALU.subtract).then_inc(done, 1)

            for i in range(1, 3):
                pool.wait_ge(w_hi_ok, i + 1)
                if i == 1:
                    pool.wait_ge(w_lo_ok, 1)
                split_lo(w_lo3[:, i], stage3[:, i], w_hi3[:, i], w_lo_ok)
            pool.wait_ge(rt_hi_ok, 1)
            split_lo(rt_lo[:, :, :], rt_raw[:, :, :], rt_hi[:, :, :], rt_lo_ok)
            pool.wait_ge(small_in, 48)
            for t in range(NT):
                pool.wait_ge(xn_ready, t + 1)
                pool.tensor_tensor(h[:, t, :], h[:, t, :], b_u[:, :], ALU.add).then_inc(hb_ok, 1)
            for g in range(NG):
                pool.wait_ge(wu_hi_ok, g + 1)
                split_lo(wu_lo[:, g, :], wu_raw[:, g, :], wu_hi[:, g, :], wu_lo_ok)

            def item_low(j, b):
                pool.wait_ge(gu_hi_ok, j + 1)
                split_lo(ex_lo[:, b % 2, 0:GU], raw[:, b, 0:GU], ex_hi[:, b % 2, 0:GU], gu_lo_ok)
                pool.wait_ge(dn_hi_ok, j + 1)
                split_lo(ex_lo[:, b % 2, GU:ITEM], raw[:, b, GU:ITEM], ex_hi[:, b % 2, GU:ITEM], dn_lo_ok)

            for j in range(SHARED):
                item_low(j, j)
            pool.wait_ge(ctl_ok, 1)
            n = pool.value_load(ctl[0:1, CTL_N:CTL_N + 1], min_val=TOP_K, max_val=E)
            for j in range(SHARED, PEEL):
                item_low(j, j)
            with pool.Fori(PEEL, PEEL + E, RAW) as i:
                for b in range(RAW):
                    with pool.If(n > i + (b - SHARED)):
                        item_low(i + b, b)

        @block.vector
        def _(dve):
            steps = [0]

            def done(ins):
                steps[0] += 1
                ins.then_inc(step, 1)

            def settle():
                dve.wait_ge(step, steps[0])

            def tt(out, a, b, op):
                return dve.tensor_tensor(out, a, b, op)

            dve.wait_ge(w_hi_ok, 1)
            tt(w_lo3[:, 0], stage3[:, 0], w_hi3[:, 0].bitcast(F32), ALU.subtract).then_inc(w_lo_ok, 1)

            def layer_norm(nth):
                settle()
                for t in range(NT):
                    done(dve.bn_stats(stats[:, t, :], h[:, t, :]))
                settle()
                for t in range(NT):
                    done(dve.bn_aggr(mv[:, t, :], stats[:, t, :]))
                settle()
                done(dve.tensor_scalar(rvar[:, :], mv[:, :, 1], LN_EPS, None, ALU.add))
                settle()
                dve.reciprocal(rvar[:, :], rvar[:, :]).then_inc(rvar_ok, 1)
                dve.wait_ge(rstd_ok, nth + 1)
                for t in range(NT):
                    dve.tensor_scalar(xn[:, t, :], h[:, t, :], mv[:, t, 0:1], rstd[:, t:t + 1],
                                      ALU.subtract, ALU.mult).then_inc(xn_ready, 1)

            def xt_low(nth, bank_of):
                for t in range(NT):
                    dve.wait_ge(xt_hi_ok, nth * NT + t + 1)
                    cols = slice(t * P, (t + 1) * P)
                    src = banks[bank_of[t]][:, 0:D].rearrange("p (k n) -> p k n", k=KD)
                    tt(xt_lo[:, :, cols], src, xt_hi[:, :, cols].bitcast(F32), ALU.subtract).then_inc(xt_lo_ok, 1)

            dve.wait_ge(bias_in, 16)
            for t in range(NT):
                dve.wait_ge(tok_mm, t + 1)
                done(tt(h[:, t, :], banks[t][:, 0:D], b_tok[:, :], ALU.add))
            layer_norm(0)
            xt_low(0, X1_BANK)
            for t in range(NT):
                dve.wait_ge(v_mm, 2 * t + 2)
                dve.tensor_copy(v_sb[:, t, BANK:2 * BANK], banks[(2 * t + 1) % 4]).then_inc(v_ok_v, 1)

            def o_low(g):
                dve.wait_ge(o_hi_ok, g + 1)
                tt(o_lo[:, g, :], banks[4 + g % 2], o_hi[:, g, :].bitcast(F32), ALU.subtract).then_inc(o_lo_ok, 1)

            dve.wait_ge(const_in, 16)
            dve.wait_ge(pt_zero, 1)
            for g in range(NG):
                dve.wait_ge(sc_mm, g + 1)
                if g >= 1:
                    dve.wait_ge(pr_ok, g)
                src = score_ps[g % 2][:, :].rearrange("p (a n) -> p a n", a=A8)
                for r in range(P // BLOCK):
                    part = slice(r * BLOCK, (r + 1) * BLOCK)
                    ins = dve.scalar_tensor_tensor(out=sc[part], in0=src[part, :, part], scalar=SCORE_SCALE,
                                                   in1=mask8[part], op0=ALU.mult, op1=ALU.add)
                ins.then_inc(sc_out, 1)
                settle()
                dve.wait_ge(sc_out, g + 1)
                done(dve.tensor_reduce(mx[:, :], sc[:, :, :], AX_X, ALU.max))
                settle()
                tt(sc[:, :, :], sc[:, :, :], mx[:, :].unsqueeze(2).broadcast_to([P, A8, BLOCK]),
                   ALU.subtract).then_inc(sc_sub, 1)
                if g >= 2:
                    o_low(g - 2)
                dve.wait_ge(pr_ok, g + 1)
                done(dve.tensor_reduce(sm[:, :], pr[:, g % 2], AX_X, ALU.add))
                settle()
                done(dve.reciprocal(ri[:, :], sm[:, :]))
                settle()
                done(tt(pn[:, :, :], pr[:, g % 2], ri[:, :].unsqueeze(2).broadcast_to([P, A8, BLOCK]), ALU.mult))
                settle()
                if g >= 2:
                    dve.wait_ge(pv_mm, g - 1)
                for r in range(P // BLOCK):
                    part = slice(r * BLOCK, (r + 1) * BLOCK)
                    ins = dve.transpose(p_t[part, g % 2, :, part], pn[part])
                ins.then_inc(pt_ok, 1)
            o_low(NG - 2)
            o_low(NG - 1)

            for t in range(NT):
                dve.wait_ge(u_mm, t + 1)
                dve.wait_ge(hb_ok, t + 1)
                done(tt(h[:, t, :], banks[U_BANK[t]][:, 0:D], h[:, t, :], ALU.add))
            dve.wait_ge(xt_ps, NT)
            layer_norm(1)
            xt_low(1, X2_BANK)

            def over_experts(x):
                return x.unsqueeze(2).broadcast_to([P, NT, E])

            dve.wait_ge(small_in, 48)
            dve.wait_ge(rt_mm, 1)
            logits = banks[2][:, 0:NT * E].rearrange("p (t e) -> p t e", t=NT)
            done(dve.tensor_reduce(r4[:, 0, :], logits, AX_X, ALU.max))
            settle()
            tt(rl[:, :, :], logits, over_experts(r4[:, 0, :]), ALU.subtract).then_inc(rt_sub, 1)
            dve.wait_ge(rt_exp, 1)
            done(dve.tensor_reduce(r4[:, 1, :], re_[:, :, :], AX_X, ALU.add))
            settle()
            done(dve.reciprocal(r4[:, 2, :], r4[:, 1, :]))
            settle()
            done(tt(rw[:, :, :], re_[:, :, :], over_experts(r4[:, 2, :]), ALU.mult))
            settle()
            done(tt(corr[:, :, :], rw[:, :, :], e_bias[:, :].unsqueeze(1).broadcast_to([P, NT, E]), ALU.add))
            settle()
            for t in range(NT):
                done(dve.max(top8[:, t, :], corr[:, t, :]))
            settle()
            for t in range(NT):
                done(dve.max_index(idx8[:, t, :], top8[:, t, :], corr[:, t, :]))
            settle()
            done(dve.tensor_copy(idxf[:, :, :], idx8[:, :, :]))
            settle()
            iota = iota6.rearrange("p (k e) -> p k e", k=TOP_K)
            for t in range(NT):
                done(tt(hit[:, t], iota, idxf[:, t, 0:TOP_K].unsqueeze(2).broadcast_to([P, TOP_K, E]),
                        ALU.is_equal))
            settle()
            done(dve.tensor_reduce(chosen[:, :, :], hit[:, :, :, :].rearrange("p t k e -> p t e k"), AX_X, ALU.add))
            settle()
            done(tt(picked[:, :, :], rw[:, :, :], chosen[:, :, :], ALU.mult))
            settle()
            done(dve.tensor_reduce(r4[:, 3, :], picked[:, :, :], AX_X, ALU.add))
            settle()
            done(dve.tensor_scalar(r4[:, 4, :], r4[:, 3, :], NORM_MIN, None, ALU.max))
            settle()
            done(dve.reciprocal(r4[:, 5, :], r4[:, 4, :]))
            settle()
            tt(comb[:, :, :], picked[:, :, :], over_experts(r4[:, 5, :]), ALU.mult).then_inc(comb_ok, 1)

            def h_item(j, b, routed):
                dve.wait_ge(silu_ok, j + 1)
                gate = gate_act[:, b % 2, :]
                if routed:
                    dve.wait_ge(cb_in[b], 4 * (j - b) + (16 if b >= SHARED else 0))
                    tt(gate, gate, comb_bc[:, b, :], ALU.mult).then_inc(gc_ok, 1)
                    dve.wait_ge(gc_ok, j - SHARED + 1)
                dve.wait_ge(up_mm, j + 1)
                if not (type(j) is int and j < 2):
                    dve.wait_ge(hm_hi_ok, j - 1)
                    dve.wait_ge(hm_lo_ok, j - 1)
                tt(h_mid[:, b % 2, :], up_bank(b), gate, ALU.mult).then_inc(hm_ok, 1)
                if not (type(j) is int and j < 2):
                    dve.wait_ge(down_mm, j - 1)
                dve.wait_ge(hm_hi_ok, j + 1)
                tt(hm_lo[:, b % 2, :], h_mid[:, b % 2, :], hm_hi[:, b % 2, :].bitcast(F32),
                   ALU.subtract).then_inc(hm_lo_ok, 1)

            dve.wait_ge(ct_mm, 1)
            dve.tensor_copy(comb_t[:, :], banks[3][0:E, :]).then_inc(ct_ok, 1)
            dve.wait_ge(cnt_mm, 1)
            dve.tensor_scalar(active[:, :], banks[2][0:E, 0:1], 1.0, None, ALU.min).then_inc(act_ok, 1)
            h_item(0, 0, False)
            dve.wait_ge(pos_mm, 1)
            done(dve.tensor_copy(pos[:, :], banks[2][0:E, 1:2]))
            dve.wait_ge(act_ok, 1)
            settle()
            dve.tensor_scalar(place[:, :], slots, pos[:, :], active[:, :], ALU.is_equal,
                              ALU.mult).then_inc(place_ok, 1)
            dve.wait_ge(list_mm, 1)
            done(dve.tensor_copy(ctl[0:1, 0:LIST], banks[2][0:1, 0:LIST]))
            dve.tensor_copy(ctl[0:1, CTL_N:CTL_N + 1], banks[2][0:1, CTL_N:CTL_N + 1]).then_inc(ctl_ok, 1)
            h_item(1, 1, False)
            dve.wait_ge(h2_ps, 1)
            for k in range(KD):
                done(dve.tensor_copy(h2_t[:, k, :], banks[2 + k]))
            dve.wait_ge(ctl_ok, 1)
            n = dve.value_load(ctl[0:1, CTL_N:CTL_N + 1], min_val=TOP_K, max_val=E)
            for j in range(SHARED, PEEL):
                h_item(j, j, True)
            with dve.Fori(PEEL, PEEL + E, RAW) as i:
                for b in range(RAW):
                    with dve.If(n > i + (b - SHARED)):
                        h_item(i + b, b, True)
            dve.wait_ge(down_mm, n + SHARED)
            for m in range(KD):
                tt(o_sb[:, m, :], banks[4 + m], h2_t[:, m, :], ALU.add).then_inc(out_ok, 1)


def _constants():
    import numpy as np
    c = np.zeros((P, C_COLS), np.float32)
    c[:, C_IDENT:C_IDENT + P] = np.eye(P, dtype=np.float32)
    row = np.arange(P)[:, None] % BLOCK
    col = np.arange(BLOCK)[None, :]
    seen = (row // SEQ == col // SEQ) & (col <= row)
    c[:, C_MASK:C_MASK + MASK_COPIES * BLOCK] = np.tile(np.where(seen, 0.0, MASKED), (1, MASK_COPIES))
    c[:, C_IOTA:C_IOTA + TOP_K * 32] = np.tile(np.arange(32), TOP_K)[None]
    c[0:32, C_BEFORE:C_BEFORE + 32] = np.triu(np.ones((32, 32)), 1)
    c[0:32, C_SLOT:C_SLOT + LIST] = np.arange(LIST)[None]
    c[0:32, C_NUMBER] = np.arange(32)
    c[:, C_ONE] = 1.0
    return c


def kernel(x, L0_tok_W, L0_tok_b, L0_attn_w_q, L0_attn_w_k, L0_attn_w_v, L0_attn_w_u, L0_attn_b_u,
           L0_ffn_router_weight, L0_ffn_e_score_bias, L0_ffn_gate_up_proj, L0_ffn_down_proj,
           L0_ffn_shared_gate_w, L0_ffn_shared_up_w, L0_ffn_shared_down_w):
    import numpy as np
    import concourse.bacc as bacc
    from concourse.bass_utils import run_bass_kernel_spmd

    def rows(a):
        a = np.asarray(a)
        return np.ascontiguousarray(a.reshape(a.shape[0] // P, P, a.shape[1]))

    x = np.asarray(x)
    nb, ch, height, width = x.shape
    side = 16
    patches = x.reshape(nb, ch, height // side, side, width // side, side).transpose(0, 2, 3, 1, 4, 5)
    patches = patches.reshape(-1, ch * side * side)
    d = L0_tok_W.shape[0]

    def item(gate_up, down):
        n = gate_up.shape[0]
        gu = gate_up.transpose(0, 2, 1).reshape(n, d // P, P, 2 * P).transpose(0, 2, 1, 3).reshape(n, P, -1)
        return np.concatenate([gu, down.transpose(0, 2, 1)], axis=2)

    sg, su, sd = (np.asarray(a) for a in (L0_ffn_shared_gate_w, L0_ffn_shared_up_w, L0_ffn_shared_down_w))
    halves = sg.shape[0] // P
    shared_gu = np.concatenate([sg.reshape(halves, P, d), su.reshape(halves, P, d)], axis=1)
    shared_dn = sd.reshape(d, halves, P).transpose(1, 0, 2)
    experts = np.concatenate([item(np.asarray(L0_ffn_gate_up_proj), np.asarray(L0_ffn_down_proj)),
                              item(shared_gu, shared_dn)], axis=0)
    arrays = {
        "patches_t": rows(patches.T),
        "w_tok_t": rows(np.asarray(L0_tok_W).T),
        "b_tok_row": np.asarray(L0_tok_b)[None],
        "w_q": rows(L0_attn_w_q),
        "w_k": rows(L0_attn_w_k),
        "w_v": rows(L0_attn_w_v),
        "w_u": rows(L0_attn_w_u),
        "b_u_row": np.asarray(L0_attn_b_u)[None],
        "router_t": rows(np.asarray(L0_ffn_router_weight).T),
        "expert_bias_row": np.asarray(L0_ffn_e_score_bias)[None],
        "expert_weights": np.ascontiguousarray(experts),
        "constants": _constants(),
    }
    nc = bacc.Bacc("TRN2", target_bir_lowering=False, num_devices=1)
    args = [nc.dram_tensor(k, a.shape, F32, kind="ExternalInput").ap() for k, a in arrays.items()]
    out = nc.dram_tensor("out_t", (d // P, P, patches.shape[0]), F32, kind="ExternalOutput").ap()
    vit_block(nc, *args, out)
    r = run_bass_kernel_spmd(nc, [arrays], core_ids=[0])
    out_t = r.results[0]["out_t"]
    return np.ascontiguousarray(out_t.reshape(d, -1).T).reshape(nb, -1, d)
```

```python
from contextlib import ExitStack

import concourse.bass as bass
from concourse import mybir

P = 128
F32 = mybir.dt.float32
F32R = mybir.dt.float32r
I32 = mybir.dt.int32
U32 = mybir.dt.uint32
ALU = mybir.AluOpType
ACT = mybir.ActivationFunctionType
AX_X = mybir.AxisListType.X

BANK = 512
BLOCK = 32
SEQ = 16
HEAD = 64
TOP_K = 6
LN_EPS = 1e-5
NORM_MIN = 1e-12
MASKED = -3.0e38
MASK_COPIES = 8
LIST = 36
CTL_N = LIST
C_IDENT = 0
C_MASK = C_IDENT + P
C_IOTA = C_MASK + MASK_COPIES * BLOCK
C_BEFORE = C_IOTA + TOP_K * 32
C_SLOT = C_BEFORE + 32
C_NUMBER = C_SLOT + LIST
C_ONE = C_NUMBER + 1
C_COLS = C_ONE + 1


def vit_block(nc, xp_d, w_tok_d, b_tok_d, wq_d, wk_d, wv_d, wu_d, bu_d, router_d, ebias_d, experts_d,
              consts_d, out_d):
    KP = xp_d.shape[0]
    T = xp_d.shape[2]
    NT = T // P
    D = w_tok_d.shape[2]
    KD = D // P
    DA = wq_d.shape[2]
    NG = DA // P
    NITEM = experts_d.shape[0]
    E = router_d.shape[2]
    SHARED = NITEM - E
    EARLY = 2
    GU = KD * 2 * P
    ITEM = GU + D
    RAW = 4
    SCORE_SCALE = 1.0 / HEAD

    comb_d = nc.dram_tensor("combine_rows", [E, T], F32, kind="Internal").ap()

    with ExitStack() as ctx:
        def sb(name, shape, dt=F32):
            return ctx.enter_context(nc.sbuf_tensor(name, shape, dt))

        def sem(name):
            return ctx.enter_context(nc.semaphore(name))

        ps = [ctx.enter_context(nc.psum_tensor(f"bank{i}", [P, BANK], F32)) for i in range(2)]
        score_ps = [ctx.enter_context(nc.psum_tensor(f"score_ps{i}", [P, 2 * BANK], F32)) for i in range(2)]
        ps += [ctx.enter_context(nc.psum_tensor(f"bank{i}", [P, BANK], F32)) for i in range(6, 8)]
        banks = {0: score_ps[0][:, 0:BANK], 1: score_ps[0][:, BANK:2 * BANK],
                 2: score_ps[1][:, 0:BANK], 3: score_ps[1][:, BANK:2 * BANK],
                 4: ps[0][:, :], 5: ps[1][:, :], 6: ps[2][:, :], 7: ps[3][:, :]}

        consts = sb("consts", [P, C_COLS])
        ident = consts[:, C_IDENT:C_IDENT + P]
        mask8 = consts[:, C_MASK:C_MASK + MASK_COPIES * BLOCK].rearrange("p (a c) -> p a c", c=BLOCK)
        iota6 = consts[:, C_IOTA:C_IOTA + TOP_K * E]
        before = consts[0:E, C_BEFORE:C_BEFORE + E]
        slots = consts[0:E, C_SLOT:C_SLOT + LIST]
        number = consts[0:E, C_NUMBER:C_NUMBER + 1]
        one_col = consts[:, C_ONE:C_ONE + 1]
        eps_col = sb("eps_col", [P, 1])[:, :]
        warm = sb("warm", [P, BANK], mybir.dt.bfloat16)
        b_tok = sb("b_tok", [1, D])
        b_hi = sb("b_hi", [1, D], F32R)
        b_lo = sb("b_lo", [1, D], F32R)
        one_row = sb("one_row", [1, P])
        one_r = sb("one_r", [1, P], F32R)
        b_u = sb("b_u", [P, D])
        e_bias = sb("e_bias", [P, E])

        xp = sb("xp", [P, KP * T])
        raw = xp[:, 0:RAW * ITEM].rearrange("p (r n) -> p r n", r=RAW)
        w_tok = sb("w_tok", [P, KP, D])
        stage = sb("stage", [P, 3 * KD * DA])
        stage3 = stage[:, :].rearrange("p (w k n) -> p w k n", w=3, k=KD)
        wu_raw = stage[:, 0:KD * DA].rearrange("p (g n) -> p g n", g=NG)
        tail = KD * DA
        comb_bc = stage[:, tail:tail + RAW * T].rearrange("p (r n) -> p r n", r=RAW)
        gate_act = stage[:, tail + RAW * T:tail + (RAW + 2) * T].rearrange("p (r n) -> p r n", r=2)
        h_mid = stage[:, tail + (RAW + 2) * T:tail + (RAW + 4) * T].rearrange("p (r n) -> p r n", r=2)
        w_hi = sb("w_hi", [P, 3 * KD * DA], F32R)
        w_lo = sb("w_lo", [P, 3 * KD * DA], F32R)
        w_hi3 = w_hi[:, :].rearrange("p (w k n) -> p w k n", w=3, k=KD)
        w_lo3 = w_lo[:, :].rearrange("p (w k n) -> p w k n", w=3, k=KD)
        ex_hi = w_hi[:, 0:2 * ITEM].rearrange("p (r n) -> p r n", r=2)
        ex_lo = w_lo[:, 0:2 * ITEM].rearrange("p (r n) -> p r n", r=2)
        hm_hi = w_hi[:, tail:tail + 2 * T].rearrange("p (r n) -> p r n", r=2)
        hm_lo = w_lo[:, tail:tail + 2 * T].rearrange("p (r n) -> p r n", r=2)
        wu_hi = sb("wu_hi", [P, NG, D], F32R)
        wu_lo = sb("wu_lo", [P, NG, D], F32R)
        rt_raw = sb("rt_raw", [P, KD, E])
        rt_hi = sb("rt_hi", [P, KD, P], F32R)
        rt_lo = sb("rt_lo", [P, KD, P], F32R)

        h = sb("h", [P, NT, D])
        xn = sb("xn", [P, NT, D])
        xt_hi = sb("xt_hi", [P, KD, T], F32R)
        xt_lo = sb("xt_lo", [P, KD, T], F32R)
        stats = sb("stats", [P, NT, 6])
        mv = sb("mv", [P, NT, 2])
        std = sb("std", [P, NT + 1])
        rstd = sb("rstd", [P, NT])
        q_t = sb("q_t", [P, 2, T])
        k_t = sb("k_t", [P, 2, T])
        v_sb = sb("v_sb", [P, NT, DA])
        A8 = MASK_COPIES
        sc = sb("sc", [P, A8, BLOCK])
        pr = sb("pr", [P, 2, A8, BLOCK])
        mx = sb("mx", [P, A8])
        sm = sb("sm", [P, A8])
        ri = sb("ri", [P, A8])
        pn = sb("pn", [P, A8, BLOCK])
        p_t = sb("p_t", [P, 2, A8, P])
        o_hi = sb("o_hi", [P, NG, T], F32R)
        o_lo = sb("o_lo", [P, NG, T], F32R)
        xp_hi = o_hi[:, :, :].rearrange("p g n -> p (g n)")[:, 0:KP * T].rearrange("p (c n) -> p c n", c=KP)
        xp_lo = o_lo[:, :, :].rearrange("p g n -> p (g n)")[:, 0:KP * T].rearrange("p (c n) -> p c n", c=KP)
        wt_hi = wu_hi[:, 0:KP, :]
        wt_lo = wu_lo[:, 0:KP, :]
        xp3 = xp[:, :].rearrange("p (c n) -> p c n", c=KP)
        rl = sb("rl", [P, NT, E])
        re_ = sb("re", [P, NT, E])
        rw = sb("rw", [P, NT, E])
        corr = sb("corr", [P, NT, E])
        top8 = sb("top8", [P, NT, 8])
        idx8 = sb("idx8", [P, NT, 8], U32)
        idxf = sb("idxf", [P, NT, 8])
        chosen = sb("chosen", [P, NT, E])
        picked = sb("picked", [P, NT, E])
        comb = sb("comb", [P, NT, E])
        r4 = sb("r4", [P, 6, NT])
        active = sb("active", [E, 1])
        pos = sb("pos", [E, 1])
        b8 = sb("b8", [1, 8])
        bi8 = sb("bi8", [1, 8], U32)
        bif = sb("bif", [1, 8])
        early_row = sb("early_row", [1, EARLY, E])
        early_col = sb("early_col", [E, EARLY])
        early_sel = sb("early_sel", [E, EARLY, P])
        late = sb("late", [E, 1])
        place = sb("place", [E, LIST])
        ctl = sb("ctl", [1, CTL_N + 1], I32)
        o_sb = v_sb[:, 1, 0:KD * T].rearrange("p (k n) -> p k n", k=KD)
        logits_t = v_sb[0:E, 2, 0:T]
        comb_t = v_sb[0:E, 2, T:2 * T]
        hit = v_sb[:, 3, 0:NT * TOP_K * E].rearrange("p (t k e) -> p t k e", t=NT, k=TOP_K)

        tok_in = [sem(f"tok_in{c}") for c in range(KP)]
        const_in = sem("const_in")
        bias_in = sem("bias_in")
        ebias_in = sem("ebias_in")
        small_in = sem("small_in")
        warm_ok = sem("warm_ok")
        rt_zero = sem("rt_zero")
        one_ok = sem("one_ok")
        eps_ok = sem("eps_ok")
        b_hi_ok = sem("b_hi_ok")
        b_lo_ok = sem("b_lo_ok")
        tok_hi_ok = sem("tok_hi_ok")
        tok_lo_ok = sem("tok_lo_ok")
        early_ok = sem("early_ok")
        row_ok = sem("row_ok")
        col_mm = sem("col_mm")
        sel_ok = sem("sel_ok")
        lt_ok = sem("lt_ok")
        lt_mm = sem("lt_mm")
        cb_mm = sem("cb_mm")
        w_in = [sem(f"w_in{i}") for i in range(3)]
        wu_in = sem("wu_in")
        raw_in = [sem(f"raw_in{i}") for i in range(RAW)]
        cb_in = [sem(f"cb_in{i}") for i in range(RAW)]
        comb_out = sem("comb_out")
        tok_mm = sem("tok_mm")
        h_ready = sem("h_ready")
        var_ok = sem("var_ok")
        std_ok = sem("std_ok")
        xn_ready = sem("xn_ready")
        xt_ps = sem("xt_ps")
        xt_hi_ok = sem("xt_hi_ok")
        xt_lo_ok = sem("xt_lo_ok")
        w_hi_v = sem("w_hi_v")
        w_hi_ok = sem("w_hi_ok")
        w_lo_v = [sem(f"w_lo_v{half}") for half in range(2)]
        w_lo_q = sem("w_lo_q")
        w_lo_k = sem("w_lo_k")
        wu_hi_ok = sem("wu_hi_ok")
        wu_lo_ok = sem("wu_lo_ok")
        rt_hi_ok = sem("rt_hi_ok")
        rt_lo_ok = sem("rt_lo_ok")
        v_mm_a = sem("v_mm_a")
        v_mm_v = sem("v_mm_v")
        v_ok_a = sem("v_ok_a")
        v_ok_v = sem("v_ok_v")
        q_mm = sem("q_mm")
        k_mm = sem("k_mm")
        q_ok = sem("q_ok")
        k_ok = sem("k_ok")
        sc_mm = sem("sc_mm")
        sc_out = sem("sc_out")
        sc_sub = sem("sc_sub")
        pr_ok = sem("pr_ok")
        pt_zero = sem("pt_zero")
        pt_ok = sem("pt_ok")
        pv_mm = sem("pv_mm")
        o_hi_ok = sem("o_hi_ok")
        o_lo_ok = sem("o_lo_ok")
        hb_ok = sem("hb_ok")
        u_mm = sem("u_mm")
        step = sem("step")
        rt_mm = sem("rt_mm")
        rt_sub = sem("rt_sub")
        rt_exp = sem("rt_exp")
        comb_ok = sem("comb_ok")
        ct_mm = sem("ct_mm")
        cnt_mm = sem("cnt_mm")
        ct_ok = sem("ct_ok")
        act_ok = sem("act_ok")
        pos_mm = sem("pos_mm")
        place_ok = sem("place_ok")
        list_mm = sem("list_mm")
        ctl_ok = sem("ctl_ok")
        h2_ok = sem("h2_ok")
        gu_hi_ok = sem("gu_hi_ok")
        gu_lo_ok = sem("gu_lo_ok")
        dn_hi_ok = sem("dn_hi_ok")
        dn_lo_ok = sem("dn_lo_ok")
        gate_mm = sem("gate_mm")
        up_mm = sem("up_mm")
        silu_ok = sem("silu_ok")
        gc_ok = sem("gc_ok")
        hm_ok = sem("hm_ok")
        hm_hi_ok = sem("hm_hi_ok")
        hm_lo_ok = sem("hm_lo_ok")
        down_mm = sem("down_mm")
        out_ok = sem("out_ok")
        out_last_ok = sem("out_last_ok")
        stored = sem("stored")

        def gate_bank(j):
            return banks[0 if j % 2 == 0 else 6]

        def up_bank(j):
            return banks[1 if j % 2 == 0 else 7]

        U_BANK = [6, 7, 0, 1]
        X1_BANK = [4, 5, 6, 7]
        X2_BANK = [2, 3, 6, 7]
        PEEL = 4
        V_BANK = [0, 1, 2, 3]
        assert SHARED + EARLY == PEEL == RAW

        block = ctx.enter_context(nc.Block())

        @block.sync
        def _(sp):
            sp.dma_start(b_tok[:, :], b_tok_d).then_inc(bias_in, 16)
            sp.dma_start(e_bias[:, :], ebias_d.broadcast_to([P, E])).then_inc(ebias_in, 16)
            for c in range(KP):
                sp.dma_start(xp[:, c * T:(c + 1) * T], xp_d[c]).then_inc(tok_in[c], 16)
                sp.dma_start(w_tok[:, c, :], w_tok_d[c]).then_inc(tok_in[c], 16)
            for i, w in enumerate((wv_d, wq_d, wk_d)):
                sp.dma_start(stage3[:, i], w.rearrange("k p n -> p k n")).then_inc(w_in[i], 16)
                if i == 0:
                    sp.dma_start(consts[:, :], consts_d).then_inc(const_in, 16)
            sp.dma_start(b_u[:, :], bu_d.broadcast_to([P, D])).then_inc(small_in, 16)
            sp.dma_start(rt_raw[:, :, :], router_d.rearrange("k p n -> p k n")).then_inc(small_in, 16)
            for half in range(2):
                sp.wait_ge(w_lo_v[half], 1)
            sp.dma_start(wu_raw, wu_d.rearrange("g p n -> p g n")).then_inc(wu_in, 16)
            sp.wait_ge(tok_lo_ok, 2 * KP)

            def load_weights(e, b):
                sp.dma_start(raw[:, b, :], experts_d[bass.ds(e, 1)].rearrange("e p n -> (e p) n")
                             ).then_inc(raw_in[b], 16)

            for j in range(SHARED):
                sp.dma_start(raw[:, j, :], experts_d[E + j]).then_inc(raw_in[j], 16)
            sp.wait_ge(early_ok, 1)
            for j in range(SHARED, PEEL):
                load_weights(sp.value_load(bi8[0:1, j - SHARED:j - SHARED + 1], min_val=0, max_val=E - 1), j)
            sp.wait_ge(ct_ok, 1)
            sp.dma_start(comb_d, comb_t[:, :]).then_inc(comb_out, 16)
            sp.wait_ge(ctl_ok, 1)
            n = sp.value_load(ctl[0:1, CTL_N:CTL_N + 1], min_val=TOP_K - EARLY, max_val=E)
            sp.wait_ge(comb_out, 16)
            with sp.Fori(PEEL, PEEL + E, RAW) as i:
                with sp.If(n > i + (-PEEL - 1)):
                    for b in range(RAW):
                        with sp.If(n > i + (b - PEEL - 1)):
                            sp.wait_ge(gu_lo_ok, i + (b - RAW + 1))
                            sp.wait_ge(dn_lo_ok, i + (b - RAW + 1))
                            e = sp.value_load(ctl[0:1, bass.ds(i + (b - PEEL), 1)], min_val=0, max_val=E - 1)
                            load_weights(e, b)
                            sp.wait_ge(hm_ok, i + (b - RAW + 1))
                            sp.dma_start(comb_bc[:, b, :], comb_d[bass.ds(e, 1), :].broadcast_to([P, T])
                                         ).then_inc(cb_in[b], 16)
                    sp.nop()
            sp.wait_ge(out_ok, 1)
            sp.dma_start(out_d[0], o_sb[:, 0, :]).then_inc(stored, 16)
            sp.wait_ge(out_last_ok, 1)
            sp.dma_start(out_d[1], o_sb[:, 1, :]).then_inc(stored, 16)
            sp.wait_ge(stored, 16 * KD)

        @block.tensor
        def _(pe):
            def keep_warm(count, bank):
                for _ in range(count):
                    pe.matmul(banks[bank], warm[:, 0:P], warm[:, :], start=True, stop=True)

            pe.wait_ge(warm_ok, 1)
            keep_warm(6, 7)
            pe.wait_ge(b_hi_ok, 1)
            pe.wait_ge(one_ok, 2)
            for t in range(NT):
                pe.matmul(banks[t][:, 0:D], one_r[:, :], b_hi[:, :], start=True, stop=False)
            pe.wait_ge(b_lo_ok, 1)
            for t in range(NT):
                pe.matmul(banks[t][:, 0:D], one_r[:, :], b_lo[:, :], start=False, stop=False)
            keep_warm(2, 7)
            for c in range(KP):
                pe.wait_ge(tok_hi_ok, 2 * c + 2)
                for p in range(3):
                    if p == 1:
                        pe.wait_ge(tok_lo_ok, 2 * c + 1)
                    if p == 2:
                        pe.wait_ge(tok_lo_ok, 2 * c + 2)
                    for t in range(NT):
                        mm = pe.matmul(banks[t][:, 0:D], (xp_hi, xp_hi, xp_lo)[p][:, c, t * P:(t + 1) * P],
                                       (wt_hi, wt_lo, wt_hi)[p][:, c, :], start=False,
                                       stop=(c == KP - 1 and p == 2))
                        if c == KP - 1 and p == 2:
                            mm.then_inc(tok_mm, 1)

            def transpose_tile(nth, t, bank):
                pe.wait_ge(xn_ready, nth * NT + t + 1)
                for k in range(KD):
                    mm = pe.transpose(banks[bank][:, k * P:(k + 1) * P], xn[:, t, k * P:(k + 1) * P], ident)
                mm.then_inc(xt_ps, 1)

            def value_half(t, half):
                pe.wait_ge(xt_hi_ok, t + 1)
                pe.wait_ge(xt_lo_ok, t + 1)
                n_v = 2 * t + half
                if n_v >= 4:
                    pe.wait_ge(v_ok_a if half == 0 else v_ok_v, (n_v - 4) // 2 + 1)
                else:
                    pe.wait_ge(h_ready, n_v + 1)
                cols = slice(half * BANK, (half + 1) * BANK)
                for i in range(3 * KD):
                    k, p = i // 3, i % 3
                    xs = (xt_hi, xt_hi, xt_lo)[p][:, k, t * P:(t + 1) * P]
                    ws = (w_hi3, w_lo3, w_hi3)[p][:, 0, k, cols]
                    mm = pe.matmul(banks[V_BANK[n_v % 4]], xs, ws, start=(i == 0), stop=(i == 3 * KD - 1))
                mm.then_inc(v_mm_a if half == 0 else v_mm_v, 1)

            pe.wait_ge(row_ok, 1)
            for i in range(EARLY):
                mm = pe.matmul(banks[7][0:E, i:i + 1], early_row[:, i, :], one_row[:, 0:1], start=True, stop=True)
            mm.then_inc(col_mm, 1)
            pe.wait_ge(const_in, 16)
            keep_warm(6, 6)
            transpose_tile(0, 0, X1_BANK[0])
            transpose_tile(0, 1, X1_BANK[1])
            keep_warm(4, 6)
            pe.wait_ge(w_hi_v, 1)
            pe.wait_ge(w_lo_v[0], 1)
            value_half(0, 0)
            value_half(1, 0)
            transpose_tile(0, 2, X1_BANK[2])
            pe.wait_ge(w_hi_v, 2)
            pe.wait_ge(w_lo_v[1], 1)
            value_half(0, 1)
            value_half(1, 1)
            pe.wait_ge(sel_ok, 1)
            transpose_tile(0, 3, X1_BANK[3])
            for t in range(2, NT):
                for half in range(2):
                    value_half(t, half)

            def project(g, which, bank, done):
                cols = slice(g * P, (g + 1) * P)
                for i in range(3 * KD):
                    k, p = i // 3, i % 3
                    ws = (w_hi3, w_hi3, w_lo3)[p][:, which, k, cols]
                    xs = (xt_hi, xt_lo, xt_hi)[p][:, k, :]
                    mm = pe.matmul(banks[bank], ws, xs, start=(i == 0), stop=(i == 3 * KD - 1))
                mm.then_inc(done, 1)

            def scores(g):
                pe.wait_ge(q_ok, g + 1)
                pe.wait_ge(k_ok, g + 1)
                if g < 2:
                    pe.wait_ge(v_ok_a, NT)
                    pe.wait_ge(v_ok_v, NT)
                else:
                    pe.wait_ge(sc_out, g - 1)
                for t in range(NT):
                    for a in range(2):
                        rows = slice(HEAD * a, HEAD * (a + 1))
                        mm = pe.matmul(score_ps[g % 2][:, (a * NT + t) * P:(a * NT + t + 1) * P],
                                       q_t[rows, g % 2, t * P:(t + 1) * P],
                                       k_t[rows, g % 2, t * P:(t + 1) * P], start=True, stop=True)
                mm.then_inc(sc_mm, 1)

            def values(g):
                pe.wait_ge(pt_ok, g + 1)
                if g < 2:
                    pe.wait_ge(xt_lo_ok, NT)
                else:
                    pe.wait_ge(o_lo_ok, g - 1)
                for a in range(2):
                    for t in range(NT):
                        mm = pe.matmul(banks[4 + g % 2][HEAD * a:HEAD * (a + 1), t * P:(t + 1) * P],
                                       v_sb[:, t, (2 * g + a) * HEAD:(2 * g + a + 1) * HEAD],
                                       p_t[:, g % 2, a * NT + t, :], start=True, stop=True)
                mm.then_inc(pv_mm, 1)

            def output(g, tiles=range(NT)):
                pe.wait_ge(o_hi_ok, g + 1)
                pe.wait_ge(o_lo_ok, g + 1)
                pe.wait_ge(wu_hi_ok, g + 1)
                pe.wait_ge(wu_lo_ok, g + 1)
                for t in tiles:
                    for p in range(3):
                        os_ = (o_hi, o_hi, o_lo)[p][:, g, t * P:(t + 1) * P]
                        ws = (wu_hi, wu_lo, wu_hi)[p][:, g, :]
                        mm = pe.matmul(banks[U_BANK[t]][:, 0:D], os_, ws, start=(g == 0 and p == 0),
                                       stop=(g == NG - 1 and p == 2))
                    if g == NG - 1:
                        mm.then_inc(u_mm, 1)

            pe.wait_ge(w_hi_ok, 2)
            pe.wait_ge(w_lo_q, 1)
            pe.wait_ge(w_lo_k, 1)
            for s in range(NG + 2):
                if s < NG:
                    if s >= 1:
                        pe.wait_ge(q_ok, s)
                    project(s, 1, 6, q_mm)
                    if s >= 1:
                        pe.wait_ge(k_ok, s)
                    project(s, 2, 7, k_mm)
                if 1 <= s <= NG:
                    scores(s - 1)
                if s == NG:
                    pe.wait_ge(q_ok, NG)
                    pe.wait_ge(k_ok, NG)
                    pe.wait_ge(sc_out, NG - 1)
                    for g in range(NG - 2):
                        output(g)
                if s >= 2:
                    values(s - 2)
            output(NG - 2)
            for t in range(NT):
                output(NG - 1, [t])

            pe.wait_ge(sc_out, NG)
            keep_warm(8, 3)
            pe.wait_ge(o_lo_ok, NG)

            def add_residual(t):
                pe.wait_ge(h2_ok, t + 1)
                for k in range(KD):
                    pe.matmul(banks[4 + k][:, t * P:(t + 1) * P], h[:, t, k * P:(k + 1) * P], ident,
                              start=(t == 0), stop=False, skip_group_check=True)

            add_residual(0)
            transpose_tile(1, 0, X2_BANK[0])
            add_residual(1)
            transpose_tile(1, 1, X2_BANK[1])
            add_residual(2)
            transpose_tile(1, 2, X2_BANK[2])
            add_residual(3)
            transpose_tile(1, 3, X2_BANK[3])

            pe.wait_ge(rt_hi_ok, 1)
            pe.wait_ge(rt_lo_ok, 1)
            pe.wait_ge(xt_hi_ok, 2 * NT)
            pe.wait_ge(xt_lo_ok, 2 * NT)
            for i in range(3 * KD):
                k, p = i // 3, i % 3
                mm = pe.matmul(banks[2], (rt_hi, rt_hi, rt_lo)[p][:, k, :], (xt_hi, xt_lo, xt_hi)[p][:, k, :],
                               start=(i == 0), stop=(i == 3 * KD - 1))
            mm.then_inc(rt_mm, 1)

            def half_item(j, b, half, bank, done):
                for i in range(3 * KD):
                    k, p = i // 3, i % 3
                    at = k * 2 * P + half * P
                    ws = (ex_hi, ex_hi, ex_lo)[p][:, b % 2, at:at + P]
                    xs = (xt_hi, xt_lo, xt_hi)[p][:, k, :]
                    mm = pe.matmul(bank, ws, xs, start=(i == 0), stop=(i == 3 * KD - 1))
                mm.then_inc(done, 1)

            def gate(j, b):
                pe.wait_ge(gu_hi_ok, j + 1)
                pe.wait_ge(gu_lo_ok, j + 1)
                if not (type(j) is int and j < 2):
                    pe.wait_ge(silu_ok, j - 1)
                half_item(j, b, 0, gate_bank(b), gate_mm)

            def up(j, b):
                if not (type(j) is int and j < 2):
                    pe.wait_ge(hm_ok, j - 1)
                half_item(j, b, 1, up_bank(b), up_mm)

            def down(j, b):
                pe.wait_ge(dn_hi_ok, j + 1)
                pe.wait_ge(dn_lo_ok, j + 1)
                pe.wait_ge(hm_hi_ok, j + 1)
                for p in range(3):
                    if p == 2:
                        pe.wait_ge(hm_lo_ok, j + 1)
                    for m in range(KD):
                        ws = (ex_hi, ex_lo, ex_hi)[p][:, b % 2, GU + m * P:GU + (m + 1) * P]
                        hs = (hm_hi, hm_hi, hm_lo)[p][:, b % 2, :]
                        mm = pe.matmul(banks[4 + m], ws, hs, start=False, stop=(p == 2),
                                       skip_group_check=True)
                mm.then_inc(down_mm, 1)

            gate(0, 0)
            pe.wait_ge(lt_ok, 1)
            for t in range(NT):
                mm = pe.transpose(banks[3][:, t * E:(t + 1) * E], logits_t[:, t * P:(t + 1) * P],
                                  consts[0:E, C_IDENT:C_IDENT + E])
            mm.then_inc(lt_mm, 1)
            up(0, 0)
            gate(1, 1)
            up(1, 1)
            down(0, 0)
            gate(2, 2)
            up(2, 2)
            pe.wait_ge(comb_ok, 1)
            for t in range(NT):
                mm = pe.transpose(banks[3][0:E, t * P:(t + 1) * P], comb[:, t, :], ident)
            mm.then_inc(ct_mm, 1)
            for t in range(NT):
                mm = pe.matmul(banks[2][0:E, 0:1], chosen[:, t, :], one_col, start=(t == 0), stop=(t == NT - 1))
            mm.then_inc(cnt_mm, 1)
            down(1, 1)
            pe.wait_ge(act_ok, 1)
            pe.matmul(banks[2][0:E, 1:2], before, active[:, :], start=True, stop=True).then_inc(pos_mm, 1)
            pe.wait_ge(ct_ok, 1)
            pe.matmul(banks[3], early_sel[:, 0, :], comb_t[:, :], start=True, stop=True).then_inc(cb_mm, 1)
            gate(3, 3)
            pe.wait_ge(place_ok, 1)
            pe.matmul(banks[2][0:1, 0:LIST], number, place[:, :], start=True, stop=True)
            pe.matmul(banks[2][0:1, CTL_N:CTL_N + 1], active[:, :], one_col[0:E, :], start=True,
                      stop=True).then_inc(list_mm, 1)
            up(3, 3)
            pe.wait_ge(ctl_ok, 1)
            pe.matmul(banks[2], early_sel[:, 1, :], comb_t[:, :], start=True, stop=True).then_inc(cb_mm, 1)
            n = pe.value_load(ctl[0:1, CTL_N:CTL_N + 1], min_val=TOP_K - EARLY, max_val=E)
            down(2, 2)
            with pe.Fori(PEEL, PEEL + E, RAW) as i:
                with pe.If(n > i + (-PEEL - 1)):
                    for b in range(RAW):
                        with pe.If(n > i + (b - PEEL)):
                            gate(i + b, b)
                            up(i + b, b)
                        with pe.If(n > i + (b - PEEL - 1)):
                            down(i + (b - 1), (b - 1) % RAW)
                    pe.nop()

        @block.scalar
        def _(act):
            def split_hi(dst, src, done):
                nc.scalar.activation(dst, src, ACT.Copy).then_inc(done, 1)

            act.wait_ge(bias_in, 16)
            split_hi(b_hi[:, :], b_tok[:, :], b_hi_ok)
            act.wait_ge(one_ok, 1)
            split_hi(one_r[:, :], one_row[:, :], one_ok)
            for c in range(KP):
                act.wait_ge(tok_in[c], 32)
                split_hi(wt_hi[:, c, :], w_tok[:, c, :], tok_hi_ok)
                split_hi(xp_hi[:, c, :], xp3[:, c, :], tok_hi_ok)
            act.wait_ge(eps_ok, 1)
            nc.scalar.activation(std[:, NT:NT + 1], eps_col, ACT.Sqrt)

            def root(nth, t):
                act.wait_ge(var_ok, nth * NT + t + 1)
                nc.scalar.activation(std[:, t:t + 1], mv[:, t, 1:2], ACT.Sqrt, bias=eps_col).then_inc(std_ok, 1)

            def xt_high(nth, t, bank):
                act.wait_ge(xt_ps, nth * NT + t + 1)
                src = banks[bank][:, 0:D].rearrange("p (k n) -> p k n", k=KD)
                split_hi(xt_hi[:, :, t * P:(t + 1) * P], src, xt_hi_ok)

            def h_copy(t):
                act.wait_ge(xn_ready, t + 1)
                nc.scalar.activation(h[:, t, :], banks[t][:, 0:D], ACT.Copy).then_inc(h_ready, 1)

            def wv_high(half):
                act.wait_ge(w_in[0], 16)
                cols = slice(half * BANK, (half + 1) * BANK)
                split_hi(w_hi3[:, 0, :, cols], stage3[:, 0, :, cols], w_hi_v)

            wv_high(0)
            wv_high(1)
            root(0, 0)
            root(0, 1)
            h_copy(0)
            root(0, 2)
            xt_high(0, 0, X1_BANK[0])
            root(0, 3)
            xt_high(0, 1, X1_BANK[1])
            h_copy(1)
            h_copy(2)
            xt_high(0, 2, X1_BANK[2])
            h_copy(3)
            act.wait_ge(w_in[1], 16)
            split_hi(w_hi3[:, 1], stage3[:, 1], w_hi_ok)

            def v_copy(t):
                act.wait_ge(v_mm_a, t + 1)
                nc.scalar.activation(v_sb[:, t, 0:BANK], banks[V_BANK[(2 * t) % 4]], ACT.Copy).then_inc(v_ok_a, 1)

            v_copy(0)
            act.wait_ge(w_in[2], 16)
            split_hi(w_hi3[:, 2], stage3[:, 2], w_hi_ok)
            xt_high(0, 3, X1_BANK[3])
            for t in range(1, NT):
                v_copy(t)
            act.wait_ge(small_in, 32)
            act.wait_ge(rt_zero, 1)
            split_hi(rt_hi[:, :, 0:E], rt_raw[:, :, :], rt_hi_ok)

            def o_high(g):
                act.wait_ge(pv_mm, g + 1)
                split_hi(o_hi[:, g, :], banks[4 + g % 2], o_hi_ok)

            for s in range(NG + 2):
                if s < NG:
                    if s >= 2:
                        act.wait_ge(sc_mm, s - 1)
                    act.wait_ge(q_mm, s + 1)
                    nc.scalar.activation(q_t[:, s % 2, :], banks[6], ACT.Copy).then_inc(q_ok, 1)
                    act.wait_ge(k_mm, s + 1)
                    nc.scalar.activation(k_t[:, s % 2, :], banks[7], ACT.Copy).then_inc(k_ok, 1)
                if 1 <= s <= NG:
                    g = s - 1
                    if g == 0:
                        act.wait_ge(wu_in, 16)
                    split_hi(wu_hi[:, g, :], wu_raw[:, g, :], wu_hi_ok)
                    act.wait_ge(sc_sub, g + 1)
                    nc.scalar.activation(pr[:, g % 2], sc[:, :, :], ACT.Exp).then_inc(pr_ok, 1)
                if s >= 2:
                    o_high(s - 2)

            def gate_up_high(j, b):
                act.wait_ge(raw_in[b], 4 * (j - b) + 16)
                if not (type(j) is int and j < 2):
                    act.wait_ge(up_mm, j - 1)
                split_hi(ex_hi[:, b % 2, 0:GU], raw[:, b, 0:GU], gu_hi_ok)

            def down_high(j, b):
                if not (type(j) is int and j < 2):
                    act.wait_ge(down_mm, j - 1)
                split_hi(ex_hi[:, b % 2, GU:ITEM], raw[:, b, GU:ITEM], dn_hi_ok)

            def silu(j, b):
                act.wait_ge(gate_mm, j + 1)
                if not (type(j) is int and j < 2):
                    act.wait_ge(hm_ok, j - 1)
                nc.scalar.activation(gate_act[:, b % 2, :], gate_bank(b), ACT.Silu).then_inc(silu_ok, 1)

            def h_high(j, b):
                act.wait_ge(hm_ok, j + 1)
                if not (type(j) is int and j < 2):
                    act.wait_ge(down_mm, j - 1)
                split_hi(hm_hi[:, b % 2, :], h_mid[:, b % 2, :], hm_hi_ok)

            act.wait_ge(v_mm_a, NT)
            act.wait_ge(v_mm_v, NT)
            for j in range(SHARED):
                gate_up_high(j, j)
                down_high(j, j)
            for t in range(NT):
                root(1, t)
                if t >= 2:
                    xt_high(1, t - 2, X2_BANK[t - 2])
            for t in range(2, NT):
                xt_high(1, t, X2_BANK[t])
            act.wait_ge(rt_mm, 1)
            nc.scalar.activation(logits_t[:, :], banks[2][0:E, :], ACT.Copy).then_inc(lt_ok, 1)
            act.wait_ge(rt_sub, 1)
            nc.scalar.activation(re_[:, :, :], rl[:, :, :], ACT.Exp).then_inc(rt_exp, 1)
            silu(0, 0)
            gate_up_high(2, 2)
            h_high(0, 0)
            silu(1, 1)
            gate_up_high(3, 3)
            h_high(1, 1)
            down_high(2, 2)
            silu(2, 2)
            h_high(2, 2)
            down_high(3, 3)
            act.wait_ge(ctl_ok, 1)
            n = act.value_load(ctl[0:1, CTL_N:CTL_N + 1], min_val=TOP_K - EARLY, max_val=E)
            with act.Fori(PEEL, PEEL + E, RAW) as i:
                with act.If(n > i + (-PEEL - 1)):
                    for b in range(RAW):
                        with act.If(n > i + (b - PEEL - 1)):
                            gate_up_high(i + b, b)
                            silu(i + (b - 1), (b - 1) % RAW)
                            h_high(i + (b - 1), (b - 1) % RAW)
                            down_high(i + b, b)
                    act.nop()
            act.wait_ge(down_mm, n + PEEL)
            nc.scalar.activation(o_sb[:, 1, :], banks[5], ACT.Copy).then_inc(out_last_ok, 1)

        @block.gpsimd
        def _(pool):
            pool.memset(p_t[:, :, :, :], 0.0).then_inc(pt_zero, 1)

            def split_lo(dst, src, hi, done):
                pool.tensor_tensor(dst, src, hi.bitcast(F32), ALU.subtract).then_inc(done, 1)

            for w in (rt_hi, rt_lo):
                ins = pool.memset(w[:, :, :].bitcast(F32), 0.0)
            ins.then_inc(rt_zero, 1)
            pool.wait_ge(w_hi_v, 2)
            second = slice(BANK, 2 * BANK)
            split_lo(w_lo3[:, 0, :, second], stage3[:, 0, :, second], w_hi3[:, 0, :, second], w_lo_v[1])
            pool.wait_ge(w_hi_ok, 1)
            split_lo(w_lo3[:, 1], stage3[:, 1], w_hi3[:, 1], w_lo_q)
            pool.wait_ge(rt_hi_ok, 1)
            split_lo(rt_lo[:, :, 0:E], rt_raw[:, :, :], rt_hi[:, :, 0:E], rt_lo_ok)
            pool.wait_ge(small_in, 32)
            for t in range(NT):
                pool.wait_ge(h_ready, t + 1)
                pool.tensor_tensor(h[:, t, :], h[:, t, :], b_u[:, :], ALU.add).then_inc(hb_ok, 1)
            for g in range(NG):
                pool.wait_ge(wu_hi_ok, g + 1)
                split_lo(wu_lo[:, g, :], wu_raw[:, g, :], wu_hi[:, g, :], wu_lo_ok)

            def item_low(j, b):
                pool.wait_ge(gu_hi_ok, j + 1)
                split_lo(ex_lo[:, b % 2, 0:GU], raw[:, b, 0:GU], ex_hi[:, b % 2, 0:GU], gu_lo_ok)
                pool.wait_ge(dn_hi_ok, j + 1)
                split_lo(ex_lo[:, b % 2, GU:ITEM], raw[:, b, GU:ITEM], ex_hi[:, b % 2, GU:ITEM], dn_lo_ok)

            for j in range(PEEL):
                item_low(j, j)
            pool.wait_ge(ctl_ok, 1)
            n = pool.value_load(ctl[0:1, CTL_N:CTL_N + 1], min_val=TOP_K - EARLY, max_val=E)
            with pool.Fori(PEEL, PEEL + E, RAW) as i:
                with pool.If(n > i + (-PEEL)):
                    for b in range(RAW):
                        with pool.If(n > i + (b - PEEL)):
                            item_low(i + b, b)
                    pool.nop()

        @block.vector
        def _(dve):
            steps = [0]

            def done(ins):
                steps[0] += 1
                ins.then_inc(step, 1)

            def settle():
                dve.wait_ge(step, steps[0])

            def tt(out, a, b, op):
                return dve.tensor_tensor(out, a, b, op)

            dve.memset(warm[:, :], 0.0).then_inc(warm_ok, 1)
            dve.memset(one_row[:, :], 1.0).then_inc(one_ok, 1)
            dve.memset(eps_col, LN_EPS).then_inc(eps_ok, 1)
            dve.wait_ge(ebias_in, 16)
            done(dve.max(b8[:, :], e_bias[0:1, :]))
            settle()
            dve.max_index(bi8[:, :], b8[:, :], e_bias[0:1, :]).then_inc(early_ok, 1)
            dve.wait_ge(early_ok, 1)
            done(dve.tensor_copy(bif[:, :], bi8[:, :]))
            dve.wait_ge(b_hi_ok, 1)
            tt(b_lo[:, :], b_tok[:, :], b_hi[:, :].bitcast(F32), ALU.subtract).then_inc(b_lo_ok, 1)
            for c in range(KP):
                dve.wait_ge(tok_hi_ok, 2 * c + 1)
                tt(wt_lo[:, c, :], w_tok[:, c, :], wt_hi[:, c, :].bitcast(F32), ALU.subtract).then_inc(tok_lo_ok, 1)
                dve.wait_ge(tok_hi_ok, 2 * c + 2)
                tt(xp_lo[:, c, :], xp3[:, c, :], xp_hi[:, c, :].bitcast(F32), ALU.subtract).then_inc(tok_lo_ok, 1)
            dve.wait_ge(const_in, 16)
            settle()
            for i in range(EARLY):
                ins = dve.tensor_scalar(early_row[:, i, :], iota6[0:1, 0:E], bif[:, i:i + 1], None, ALU.is_equal)
            ins.then_inc(row_ok, 1)

            dve.wait_ge(w_hi_v, 1)
            first = slice(0, BANK)
            tt(w_lo3[:, 0, :, first], stage3[:, 0, :, first], w_hi3[:, 0, :, first].bitcast(F32),
               ALU.subtract).then_inc(w_lo_v[0], 1)

            def statistics(nth, t, src):
                done(dve.bn_stats(stats[:, t, :], src))
                settle()
                dve.bn_aggr(mv[:, t, :], stats[:, t, :]).then_inc(var_ok, 1)

            def normalise(nth, t, src):
                dve.wait_ge(std_ok, nth * NT + t + 1)
                done(dve.reciprocal(rstd[:, t:t + 1], std[:, t:t + 1]))
                settle()
                dve.tensor_scalar(xn[:, t, :], src, mv[:, t, 0:1], rstd[:, t:t + 1],
                                  ALU.subtract, ALU.mult).then_inc(xn_ready, 1)

            def xt_low(nth, t, bank):
                dve.wait_ge(xt_hi_ok, nth * NT + t + 1)
                cols = slice(t * P, (t + 1) * P)
                src = banks[bank][:, 0:D].rearrange("p (k n) -> p k n", k=KD)
                tt(xt_lo[:, :, cols], src, xt_hi[:, :, cols].bitcast(F32), ALU.subtract).then_inc(xt_lo_ok, 1)

            def stats1(t):
                dve.wait_ge(tok_mm, t + 1)
                statistics(0, t, banks[t][:, 0:D])

            def norm1(t):
                normalise(0, t, banks[t][:, 0:D])

            stats1(0)
            stats1(1)
            norm1(0)
            norm1(1)
            stats1(2)
            xt_low(0, 0, X1_BANK[0])
            stats1(3)
            norm1(2)
            xt_low(0, 1, X1_BANK[1])
            norm1(3)
            dve.wait_ge(col_mm, 1)
            done(dve.tensor_copy(early_col[:, :], banks[7][0:E, 0:EARLY]))
            settle()
            done(dve.tensor_tensor(late[:, :], early_col[:, 0:1], early_col[:, 1:2], ALU.add))
            settle()
            done(dve.tensor_scalar(late[:, :], late[:, :], -1.0, 1.0, ALU.mult, ALU.add))
            dve.tensor_copy(early_sel[:, :, :], early_col[:, :].unsqueeze(2).broadcast_to([E, EARLY, P])
                            ).then_inc(sel_ok, 1)

            def v_copy(t):
                dve.wait_ge(v_mm_v, t + 1)
                dve.tensor_copy(v_sb[:, t, BANK:2 * BANK], banks[V_BANK[(2 * t + 1) % 4]]).then_inc(v_ok_v, 1)

            xt_low(0, 2, X1_BANK[2])
            v_copy(0)
            xt_low(0, 3, X1_BANK[3])
            v_copy(1)
            dve.wait_ge(w_hi_ok, 2)
            tt(w_lo3[:, 2], stage3[:, 2], w_hi3[:, 2].bitcast(F32), ALU.subtract).then_inc(w_lo_k, 1)
            for t in range(2, NT):
                v_copy(t)

            def o_low(g):
                dve.wait_ge(o_hi_ok, g + 1)
                tt(o_lo[:, g, :], banks[4 + g % 2], o_hi[:, g, :].bitcast(F32), ALU.subtract).then_inc(o_lo_ok, 1)

            dve.wait_ge(const_in, 16)
            dve.wait_ge(pt_zero, 1)
            for g in range(NG):
                dve.wait_ge(sc_mm, g + 1)
                if g >= 1:
                    dve.wait_ge(pr_ok, g)
                src = score_ps[g % 2][:, :].rearrange("p (a n) -> p a n", a=A8)
                for r in range(P // BLOCK):
                    part = slice(r * BLOCK, (r + 1) * BLOCK)
                    ins = dve.scalar_tensor_tensor(out=sc[part], in0=src[part, :, part], scalar=SCORE_SCALE,
                                                   in1=mask8[part], op0=ALU.mult, op1=ALU.add)
                ins.then_inc(sc_out, 1)
                settle()
                dve.wait_ge(sc_out, g + 1)
                done(dve.tensor_reduce(mx[:, :], sc[:, :, :], AX_X, ALU.max))
                settle()
                tt(sc[:, :, :], sc[:, :, :], mx[:, :].unsqueeze(2).broadcast_to([P, A8, BLOCK]),
                   ALU.subtract).then_inc(sc_sub, 1)
                if g >= 2:
                    o_low(g - 2)
                dve.wait_ge(pr_ok, g + 1)
                done(dve.tensor_reduce(sm[:, :], pr[:, g % 2], AX_X, ALU.add))
                settle()
                done(dve.reciprocal(ri[:, :], sm[:, :]))
                settle()
                done(tt(pn[:, :, :], pr[:, g % 2], ri[:, :].unsqueeze(2).broadcast_to([P, A8, BLOCK]), ALU.mult))
                settle()
                if g >= 2:
                    dve.wait_ge(pv_mm, g - 1)
                for r in range(P // BLOCK):
                    part = slice(r * BLOCK, (r + 1) * BLOCK)
                    ins = dve.transpose(p_t[part, g % 2, :, part], pn[part])
                ins.then_inc(pt_ok, 1)
            o_low(NG - 2)
            o_low(NG - 1)

            def stats2(t):
                dve.wait_ge(u_mm, t + 1)
                dve.wait_ge(hb_ok, t + 1)
                tt(h[:, t, :], banks[U_BANK[t]][:, 0:D], h[:, t, :], ALU.add).then_inc(h2_ok, 1)
                dve.wait_ge(h2_ok, t + 1)
                statistics(1, t, h[:, t, :])

            def norm2(t):
                normalise(1, t, h[:, t, :])

            stats2(0)
            stats2(1)
            norm2(0)
            stats2(2)
            norm2(1)
            xt_low(1, 0, X2_BANK[0])
            stats2(3)
            norm2(2)
            xt_low(1, 1, X2_BANK[1])
            norm2(3)
            xt_low(1, 2, X2_BANK[2])
            xt_low(1, 3, X2_BANK[3])

            def h_make(j, b, row=None):
                dve.wait_ge(silu_ok, j + 1)
                act_g = gate_act[:, b % 2, :]
                if row is not None:
                    tt(act_g, act_g, row, ALU.mult).then_inc(gc_ok, 1)
                    dve.wait_ge(gc_ok, j - SHARED + 1)
                dve.wait_ge(up_mm, j + 1)
                if not (type(j) is int and j < 2):
                    dve.wait_ge(hm_hi_ok, j - 1)
                    dve.wait_ge(hm_lo_ok, j - 1)
                tt(h_mid[:, b % 2, :], up_bank(b), act_g, ALU.mult).then_inc(hm_ok, 1)

            def h_low(j, b):
                if not (type(j) is int and j < 2):
                    dve.wait_ge(down_mm, j - 1)
                dve.wait_ge(hm_hi_ok, j + 1)
                tt(hm_lo[:, b % 2, :], h_mid[:, b % 2, :], hm_hi[:, b % 2, :].bitcast(F32),
                   ALU.subtract).then_inc(hm_lo_ok, 1)

            def over_experts(x):
                return x.unsqueeze(2).broadcast_to([P, NT, E])

            dve.wait_ge(lt_mm, 1)
            logits = banks[3][:, 0:NT * E].rearrange("p (t e) -> p t e", t=NT)
            done(dve.tensor_reduce(r4[:, 0, :], logits, AX_X, ALU.max))
            settle()
            tt(rl[:, :, :], logits, over_experts(r4[:, 0, :]), ALU.subtract).then_inc(rt_sub, 1)
            dve.wait_ge(rt_exp, 1)
            done(dve.tensor_reduce(r4[:, 1, :], re_[:, :, :], AX_X, ALU.add))
            settle()
            done(dve.reciprocal(r4[:, 2, :], r4[:, 1, :]))
            settle()
            done(tt(rw[:, :, :], re_[:, :, :], over_experts(r4[:, 2, :]), ALU.mult))
            settle()
            done(tt(corr[:, :, :], rw[:, :, :], e_bias[:, :].unsqueeze(1).broadcast_to([P, NT, E]), ALU.add))
            settle()
            for t in range(NT):
                done(dve.max(top8[:, t, :], corr[:, t, :]))
            settle()
            for t in range(NT):
                done(dve.max_index(idx8[:, t, :], top8[:, t, :], corr[:, t, :]))
            settle()
            done(dve.tensor_copy(idxf[:, :, :], idx8[:, :, :]))
            settle()
            h_make(0, 0)
            iota = iota6.rearrange("p (k e) -> p k e", k=TOP_K)
            for t in range(NT):
                done(tt(hit[:, t], iota, idxf[:, t, 0:TOP_K].unsqueeze(2).broadcast_to([P, TOP_K, E]),
                        ALU.is_equal))
            settle()
            done(dve.tensor_reduce(chosen[:, :, :], hit[:, :, :, :].rearrange("p t k e -> p t e k"), AX_X, ALU.add))
            h_low(0, 0)
            settle()
            done(tt(picked[:, :, :], rw[:, :, :], chosen[:, :, :], ALU.mult))
            settle()
            done(dve.tensor_reduce(r4[:, 3, :], picked[:, :, :], AX_X, ALU.add))
            settle()
            done(dve.tensor_scalar(r4[:, 4, :], r4[:, 3, :], NORM_MIN, None, ALU.max))
            settle()
            done(dve.reciprocal(r4[:, 5, :], r4[:, 4, :]))
            settle()
            tt(comb[:, :, :], picked[:, :, :], over_experts(r4[:, 5, :]), ALU.mult).then_inc(comb_ok, 1)

            h_make(1, 1)
            dve.wait_ge(ct_mm, 1)
            dve.tensor_copy(comb_t[:, :], banks[3][0:E, :]).then_inc(ct_ok, 1)
            dve.wait_ge(cnt_mm, 1)
            dve.tensor_scalar(active[:, :], banks[2][0:E, 0:1], 1.0, late[:, :], ALU.min, ALU.mult).then_inc(act_ok, 1)
            h_low(1, 1)
            dve.wait_ge(pos_mm, 1)
            done(dve.tensor_copy(pos[:, :], banks[2][0:E, 1:2]))
            dve.wait_ge(act_ok, 1)
            settle()
            dve.tensor_scalar(place[:, :], slots, pos[:, :], active[:, :], ALU.is_equal,
                              ALU.mult).then_inc(place_ok, 1)
            dve.wait_ge(cb_mm, 1)
            h_make(2, 2, banks[3])
            dve.wait_ge(list_mm, 1)
            dve.tensor_copy(ctl[:, :], banks[2][0:1, 0:CTL_N + 1]).then_inc(ctl_ok, 1)
            h_low(2, 2)
            dve.wait_ge(ctl_ok, 1)
            n = dve.value_load(ctl[0:1, CTL_N:CTL_N + 1], min_val=TOP_K - EARLY, max_val=E)
            dve.wait_ge(cb_mm, 2)
            h_make(3, 3, banks[2])
            h_low(3, 3)
            with dve.Fori(PEEL, PEEL + E, RAW) as i:
                with dve.If(n > i + (-PEEL)):
                    for b in range(RAW):
                        with dve.If(n > i + (b - PEEL)):
                            dve.wait_ge(cb_in[b], 4 * i)
                            h_make(i + b, b, comb_bc[:, b, :])
                            h_low(i + b, b)
                    dve.nop()
            dve.wait_ge(down_mm, n + PEEL)
            dve.tensor_copy(o_sb[:, 0, :], banks[4]).then_inc(out_ok, 1)


def _constants():
    import numpy as np
    c = np.zeros((P, C_COLS), np.float32)
    c[:, C_IDENT:C_IDENT + P] = np.eye(P, dtype=np.float32)
    row = np.arange(P)[:, None] % BLOCK
    col = np.arange(BLOCK)[None, :]
    seen = (row // SEQ == col // SEQ) & (col <= row)
    c[:, C_MASK:C_MASK + MASK_COPIES * BLOCK] = np.tile(np.where(seen, 0.0, MASKED), (1, MASK_COPIES))
    c[:, C_IOTA:C_IOTA + TOP_K * 32] = np.tile(np.arange(32), TOP_K)[None]
    c[0:32, C_BEFORE:C_BEFORE + 32] = np.triu(np.ones((32, 32)), 1)
    c[0:32, C_SLOT:C_SLOT + LIST] = np.arange(LIST)[None]
    c[0:32, C_NUMBER] = np.arange(32)
    c[:, C_ONE] = 1.0
    return c


def kernel(x, L0_tok_W, L0_tok_b, L0_attn_w_q, L0_attn_w_k, L0_attn_w_v, L0_attn_w_u, L0_attn_b_u,
           L0_ffn_router_weight, L0_ffn_e_score_bias, L0_ffn_gate_up_proj, L0_ffn_down_proj,
           L0_ffn_shared_gate_w, L0_ffn_shared_up_w, L0_ffn_shared_down_w):
    import numpy as np
    import concourse.bacc as bacc
    from concourse.bass_utils import run_bass_kernel_spmd

    def rows(a):
        a = np.asarray(a)
        return np.ascontiguousarray(a.reshape(a.shape[0] // P, P, a.shape[1]))

    x = np.asarray(x)
    nb, ch, height, width = x.shape
    side = 16
    patches = x.reshape(nb, ch, height // side, side, width // side, side).transpose(0, 2, 3, 1, 4, 5)
    patches = patches.reshape(-1, ch * side * side)
    d = L0_tok_W.shape[0]

    def item(gate_up, down):
        n = gate_up.shape[0]
        gu = gate_up.transpose(0, 2, 1).reshape(n, d // P, P, 2 * P).transpose(0, 2, 1, 3).reshape(n, P, -1)
        return np.concatenate([gu, down.transpose(0, 2, 1)], axis=2)

    sg, su, sd = (np.asarray(a) for a in (L0_ffn_shared_gate_w, L0_ffn_shared_up_w, L0_ffn_shared_down_w))
    halves = sg.shape[0] // P
    shared_gu = np.concatenate([sg.reshape(halves, P, d), su.reshape(halves, P, d)], axis=1)
    shared_dn = sd.reshape(d, halves, P).transpose(1, 0, 2)
    experts = np.concatenate([item(np.asarray(L0_ffn_gate_up_proj), np.asarray(L0_ffn_down_proj)),
                              item(shared_gu, shared_dn)], axis=0)
    arrays = {
        "patches_t": rows(patches.T),
        "w_tok_t": rows(np.asarray(L0_tok_W).T),
        "b_tok_row": np.asarray(L0_tok_b)[None],
        "w_q": rows(L0_attn_w_q),
        "w_k": rows(L0_attn_w_k),
        "w_v": rows(L0_attn_w_v),
        "w_u": rows(L0_attn_w_u),
        "b_u_row": np.asarray(L0_attn_b_u)[None],
        "router_t": rows(np.asarray(L0_ffn_router_weight).T),
        "expert_bias_row": np.asarray(L0_ffn_e_score_bias)[None],
        "expert_weights": np.ascontiguousarray(experts),
        "constants": _constants(),
    }
    nc = bacc.Bacc("TRN2", target_bir_lowering=False, num_devices=1)
    args = [nc.dram_tensor(k, a.shape, F32, kind="ExternalInput").ap() for k, a in arrays.items()]
    out = nc.dram_tensor("out_t", (d // P, P, patches.shape[0]), F32, kind="ExternalOutput").ap()
    vit_block(nc, *args, out)
    r = run_bass_kernel_spmd(nc, [arrays], core_ids=[0])
    out_t = r.results[0]["out_t"]
    return np.ascontiguousarray(out_t.reshape(d, -1).T).reshape(nb, -1, d)
```

```python
from contextlib import ExitStack

import concourse.bass as bass
from concourse import mybir

P = 128
F32 = mybir.dt.float32
F32R = mybir.dt.float32r
I32 = mybir.dt.int32
ALU = mybir.AluOpType
ACT = mybir.ActivationFunctionType
AX_X = mybir.AxisListType.X

BANK = 512
BLOCK = 32
SEQ = 16
HEAD = 64
TOP_K = 6
LN_EPS = 1e-5
NORM_MIN = 1e-12
MASKED = -3.0e38
OUTDONE = 3.0e38
MASK_COPIES = 8
LIST = 52
CTL_N = LIST
C_IDENT = 0
C_MASK = C_IDENT + P
C_BEFORE = C_MASK + MASK_COPIES * BLOCK
C_SLOT = C_BEFORE + 32
C_NUMBER = C_SLOT + LIST
C_ONE = C_NUMBER + 1
C_COLS = C_ONE + 1


def vit_block(nc, xp_d, w_tok_d, b_tok_d, wq_d, wk_d, wv_d, wu_d, bu_d, router_d, ebias_d, experts_d,
              consts_d, out_d):
    KP = xp_d.shape[0]
    T = xp_d.shape[2]
    NT = T // P
    D = w_tok_d.shape[2]
    KD = D // P
    DA = wq_d.shape[2]
    NG = DA // P
    NITEM = experts_d.shape[0]
    E = router_d.shape[2]
    SHARED = NITEM - E
    LAST = 2
    EARLY = 4
    SPREAD = 2
    GU = KD * 2 * P
    ITEM = GU + D
    RAW = 4
    PEEL = SHARED + EARLY
    SPAN = 16
    SCORE_SCALE = 1.0 / HEAD

    comb_d = nc.dram_tensor("combine_rows", [E, T], F32, kind="Internal").ap()

    with ExitStack() as ctx:
        def sb(name, shape, dt=F32):
            return ctx.enter_context(nc.sbuf_tensor(name, shape, dt))

        def sem(name):
            return ctx.enter_context(nc.semaphore(name))

        ps = [ctx.enter_context(nc.psum_tensor(f"bank{i}", [P, BANK], F32)) for i in range(2)]
        score_ps = [ctx.enter_context(nc.psum_tensor(f"score_ps{i}", [P, 2 * BANK], F32)) for i in range(2)]
        ps += [ctx.enter_context(nc.psum_tensor(f"bank{i}", [P, BANK], F32)) for i in range(6, 8)]
        banks = {0: score_ps[0][:, 0:BANK], 1: score_ps[0][:, BANK:2 * BANK],
                 2: score_ps[1][:, 0:BANK], 3: score_ps[1][:, BANK:2 * BANK],
                 4: ps[0][:, :], 5: ps[1][:, :], 6: ps[2][:, :], 7: ps[3][:, :]}

        consts = sb("consts", [P, C_COLS])
        ident = consts[:, C_IDENT:C_IDENT + P]
        mask8 = consts[:, C_MASK:C_MASK + MASK_COPIES * BLOCK].rearrange("p (a c) -> p a c", c=BLOCK)
        before = consts[0:E, C_BEFORE:C_BEFORE + E]
        slots = consts[0:E, C_SLOT:C_SLOT + LIST]
        number = consts[0:E, C_NUMBER:C_NUMBER + 1]
        ones = consts[:, C_ONE:C_ONE + 1]
        eps_col = sb("eps_col", [P, 1])[:, :]
        warm = sb("warm", [P, BANK], mybir.dt.bfloat16)
        b_tok = sb("b_tok", [1, D])
        b_hi = sb("b_hi", [1, D], F32R)
        b_lo = sb("b_lo", [1, D], F32R)
        one_row = sb("one_row", [1, P])
        one_r = sb("one_r", [1, P], F32R)
        b_u = sb("b_u", [P, D])
        e_bias = sb("e_bias", [P, E])

        xp = sb("xp", [P, KP * T])
        raw = xp[:, 0:RAW * ITEM].rearrange("p (r n) -> p r n", r=RAW)
        w_tok = sb("w_tok", [P, KP, D])
        stage = sb("stage", [P, 3 * KD * DA])
        stage3 = stage[:, :].rearrange("p (w k n) -> p w k n", w=3, k=KD)
        wu_raw = stage[:, 0:KD * DA].rearrange("p (g n) -> p g n", g=NG)
        tail = KD * DA
        comb_bc = stage[:, tail:tail + RAW * T].rearrange("p (r n) -> p r n", r=RAW)
        o_full = stage[:, tail:tail + 2 * T].rearrange("p (r n) -> p r n", r=2)
        xt_full = stage[:, tail + 2 * T:tail + 2 * T + 2 * D].rearrange("p (r k n) -> p r k n", r=2, k=KD)
        gate_act = stage[:, tail + RAW * T:tail + (RAW + 2) * T].rearrange("p (r n) -> p r n", r=2)
        h_mid = stage[:, tail + (RAW + 2) * T:tail + (RAW + 4) * T].rearrange("p (r n) -> p r n", r=2)
        w_hi = sb("w_hi", [P, 3 * KD * DA], F32R)
        w_lo = sb("w_lo", [P, 3 * KD * DA], F32R)
        w_hi3 = w_hi[:, :].rearrange("p (w k n) -> p w k n", w=3, k=KD)
        w_lo3 = w_lo[:, :].rearrange("p (w k n) -> p w k n", w=3, k=KD)
        ex_hi = w_hi[:, 0:2 * ITEM].rearrange("p (r n) -> p r n", r=2)
        ex_lo = w_lo[:, 0:2 * ITEM].rearrange("p (r n) -> p r n", r=2)
        hm_hi = w_hi[:, tail:tail + 2 * T].rearrange("p (r n) -> p r n", r=2)
        hm_lo = w_lo[:, tail:tail + 2 * T].rearrange("p (r n) -> p r n", r=2)
        wu_hi = sb("wu_hi", [P, NG, D], F32R)
        wu_lo = sb("wu_lo", [P, NG, D], F32R)
        rt_raw = sb("rt_raw", [P, KD, E])
        rt_hi = sb("rt_hi", [P, KD, P], F32R)
        rt_lo = sb("rt_lo", [P, KD, P], F32R)

        h = sb("h", [P, NT, D])
        xn = sb("xn", [P, NT, D])
        xt_hi = sb("xt_hi", [P, KD, T], F32R)
        xt_lo = sb("xt_lo", [P, KD, T], F32R)
        stats = sb("stats", [P, NT, 6])
        mv = sb("mv", [P, NT, 2])
        std = sb("std", [P, NT + 1])
        rstd = sb("rstd", [P, NT])
        q_t = sb("q_t", [P, 2, T])
        k_t = sb("k_t", [P, 2, T])
        v_sb = sb("v_sb", [P, NT, DA])
        A8 = MASK_COPIES
        HALF = A8 // 2
        sc = sb("sc", [P, A8, BLOCK])
        pr = sb("pr", [P, 2, A8, BLOCK])
        mx = sb("mx", [P, A8])
        sm = sb("sm", [P, A8])
        ri = sb("ri", [P, A8])
        pn = sb("pn", [P, A8, BLOCK])
        p_t = sb("p_t", [P, 2, A8, P])
        o_hi = sb("o_hi", [P, NG, T], F32R)
        o_lo = sb("o_lo", [P, NG, T], F32R)
        xp_hi = o_hi[:, :, :].rearrange("p g n -> p (g n)")[:, 0:KP * T].rearrange("p (c n) -> p c n", c=KP)
        xp_lo = o_lo[:, :, :].rearrange("p g n -> p (g n)")[:, 0:KP * T].rearrange("p (c n) -> p c n", c=KP)
        wt_hi = wu_hi[:, 0:KP, :]
        wt_lo = wu_lo[:, 0:KP, :]
        xp3 = xp[:, :].rearrange("p (c n) -> p c n", c=KP)
        rl = sb("rl", [P, NT, E])
        re_ = sb("re", [P, NT, E])
        rw = sb("rw", [P, NT, E])
        corr = sb("corr", [P, NT, E + 8 - TOP_K])
        rest = sb("rest", [P, NT, E + 8 - TOP_K])
        top8 = sb("top8", [P, NT, 8])
        chosen = sb("chosen", [P, NT, E])
        picked = sb("picked", [P, NT, E])
        comb = sb("comb", [P, NT, E])
        r4 = sb("r4", [P, 6, NT])
        active = sb("active", [E, 1])
        pos = sb("pos", [E, 1])
        bias_col = sb("bias_col", [E, 1])
        tied = sb("tied", [E, E])
        ahead = sb("ahead", [E, E])
        rank = sb("rank", [E, 1])
        early_num = sb("early_num", [1, EARLY], I32)
        early_col = sb("early_col", [E, EARLY])
        early_sel = sb("early_sel", [E, SPREAD, P])
        late = sb("late", [E, 1])
        place = sb("place", [E, LIST])
        ctl = sb("ctl", [1, CTL_N + 1], I32)
        o_sb = v_sb[:, 1, 0:KD * T].rearrange("p (k n) -> p k n", k=KD)
        logits_t = v_sb[0:E, 2, 0:T]
        comb_t = v_sb[0:E, 2, T:2 * T]

        patches_in = [sem(f"patches_in{c}") for c in range(KP)]
        w_tok_in = [sem(f"w_tok_in{c}") for c in range(KP)]
        const_in = sem("const_in")
        bias_in = sem("bias_in")
        ebias_in = sem("ebias_in")
        small_in = sem("small_in")
        warm_ok = sem("warm_ok")
        rt_zero = sem("rt_zero")
        one_ok = sem("one_ok")
        eps_ok = sem("eps_ok")
        b_hi_ok = sem("b_hi_ok")
        b_lo_ok = sem("b_lo_ok")
        tok_hi_ok = sem("tok_hi_ok")
        tok_lo_ok = sem("tok_lo_ok")
        early_ok = sem("early_ok")
        early_mm = sem("early_mm")
        sel_ok = sem("sel_ok")
        lt_ok = sem("lt_ok")
        lt_mm = sem("lt_mm")
        cb_mm = sem("cb_mm")
        w_in = [sem(f"w_in{i}") for i in range(3)]
        wu_in = sem("wu_in")
        raw_in = [sem(f"raw_in{i}") for i in range(RAW)]
        cb_in = [sem(f"cb_in{i}") for i in range(RAW)]
        comb_out = sem("comb_out")
        tok_mm = sem("tok_mm")
        h_ready = sem("h_ready")
        var_ok = sem("var_ok")
        std_ok = sem("std_ok")
        xn_ready = sem("xn_ready")
        xt_ps = sem("xt_ps")
        xt_hi_ok = sem("xt_hi_ok")
        xt_lo_ok = sem("xt_lo_ok")
        w_hi_v = sem("w_hi_v")
        w_hi_ok = sem("w_hi_ok")
        w_lo_v = [sem(f"w_lo_v{half}") for half in range(2)]
        w_lo_q = sem("w_lo_q")
        w_lo_k = sem("w_lo_k")
        wu_hi_ok = sem("wu_hi_ok")
        wu_lo_ok = sem("wu_lo_ok")
        rt_hi_ok = sem("rt_hi_ok")
        rt_lo_ok = sem("rt_lo_ok")
        v_mm_a = sem("v_mm_a")
        v_mm_v = sem("v_mm_v")
        v_ok_a = sem("v_ok_a")
        v_ok_v = sem("v_ok_v")
        q_mm = sem("q_mm")
        k_mm = sem("k_mm")
        q_ok = sem("q_ok")
        k_ok = sem("k_ok")
        sc_mm = sem("sc_mm")
        sc_out = sem("sc_out")
        sc_sub = sem("sc_sub")
        pr_ok = sem("pr_ok")
        pt_zero = sem("pt_zero")
        pt_ok = sem("pt_ok")
        pv_mm = sem("pv_mm")
        o_hi_ok = sem("o_hi_ok")
        o_full_ok = sem("o_full_ok")
        o_lo_ok = sem("o_lo_ok")
        o_lo_last = sem("o_lo_last")
        xt_full_ok = sem("xt_full_ok")
        xt_lo_first = sem("xt_lo_first")
        hb_ok = sem("hb_ok")
        u_mm = sem("u_mm")
        step = sem("step")
        rt_mm = sem("rt_mm")
        rt_sub = sem("rt_sub")
        rt_exp = sem("rt_exp")
        chosen_ok = sem("chosen_ok")
        comb_ok = sem("comb_ok")
        ct_mm = sem("ct_mm")
        cnt_mm = sem("cnt_mm")
        ct_ok = sem("ct_ok")
        act_ok = sem("act_ok")
        pos_mm = sem("pos_mm")
        place_ok = sem("place_ok")
        list_mm = sem("list_mm")
        ctl_ok = sem("ctl_ok")
        h2_ok = sem("h2_ok")
        gu_hi_ok = sem("gu_hi_ok")
        gu_lo_ok = sem("gu_lo_ok")
        dn_hi_ok = sem("dn_hi_ok")
        dn_lo_ok = sem("dn_lo_ok")
        gate_mm = sem("gate_mm")
        up_mm = sem("up_mm")
        silu_ok = sem("silu_ok")
        gc_ok = sem("gc_ok")
        hm_ok = sem("hm_ok")
        hm_hi_ok = sem("hm_hi_ok")
        hm_lo_ok = sem("hm_lo_ok")
        down_mm = sem("down_mm")
        out_ok = sem("out_ok")
        stored = sem("stored")

        def gate_bank(j):
            return banks[0 if j % 2 == 0 else 6]

        def up_bank(j):
            return banks[1 if j % 2 == 0 else 7]

        U_BANK = [6, 7, 0, 1]
        X1_BANK = [4, 5, 6, 7]
        X2_BANK = [2, 3, 6, 7]
        LAST_BANK = [5, 4]

        def v_bank(t, half):
            return 2 * half + t % 2

        block = ctx.enter_context(nc.Block())

        @block.sync
        def _(sp):
            sp.dma_start(b_tok[:, :], b_tok_d).then_inc(bias_in, 16)
            sp.dma_start(e_bias[:, :], ebias_d.broadcast_to([P, E])).then_inc(ebias_in, 16)
            for c in range(KP):
                sp.dma_start(xp[:, c * T:(c + 1) * T], xp_d[c]).then_inc(patches_in[c], 16)
                sp.dma_start(w_tok[:, c, :], w_tok_d[c]).then_inc(w_tok_in[c], 16)
            for i, w in enumerate((wv_d, wq_d, wk_d)):
                sp.dma_start(stage3[:, i], w.rearrange("k p n -> p k n")).then_inc(w_in[i], 16)
                if i == 0:
                    sp.dma_start(consts[:, :], consts_d).then_inc(const_in, 16)
            sp.dma_start(bias_col[:, :], ebias_d.rearrange("o e -> e o")).then_inc(ebias_in, 16)
            sp.dma_start(b_u[:, :], bu_d.broadcast_to([P, D])).then_inc(small_in, 16)
            sp.dma_start(rt_raw[:, :, :], router_d.rearrange("k p n -> p k n")).then_inc(small_in, 16)
            for half in range(2):
                sp.wait_ge(w_lo_v[half], 1)
            sp.dma_start(wu_raw, wu_d.rearrange("g p n -> p g n")).then_inc(wu_in, 16)
            sp.wait_ge(tok_lo_ok, 2 * KP)

            def load_weights(e, b):
                sp.dma_start(raw[:, b, :], experts_d[bass.ds(e, 1)].rearrange("e p n -> (e p) n")
                             ).then_inc(raw_in[b], 16)

            for j in range(SHARED):
                sp.dma_start(raw[:, j, :], experts_d[E + j]).then_inc(raw_in[j], 16)
            sp.wait_ge(early_ok, 1)
            early = [sp.value_load(early_num[0:1, x:x + 1], min_val=0, max_val=E - 1) for x in range(EARLY)]
            for j in range(SHARED, PEEL):
                if j >= RAW:
                    sp.wait_ge(gu_lo_ok, j - RAW + 1)
                    sp.wait_ge(dn_lo_ok, j - RAW + 1)
                load_weights(early[j - SHARED], j % RAW)

            def load_row(e, b):
                sp.dma_start(comb_bc[:, b, :], comb_d[bass.ds(e, 1), :].broadcast_to([P, T])).then_inc(cb_in[b], 16)

            sp.wait_ge(ctl_ok, 1)
            n = sp.value_load(ctl[0:1, CTL_N:CTL_N + 1], min_val=TOP_K - EARLY, max_val=E)
            sp.wait_ge(ct_ok, 1)
            sp.dma_start(comb_d, comb_t[:, :]).then_inc(comb_out, 16)
            sp.wait_ge(comb_out, 16)
            for j in range(SHARED + SPREAD, PEEL):
                load_row(early[j - SHARED], j % RAW)
            with sp.Fori(PEEL, PEEL + E, SPAN) as first:
                with sp.If(n > first + (-PEEL - 1)):
                    with sp.Fori(0, SPAN, RAW) as i:
                        with sp.If(n > first + i + (-PEEL - 1)):
                            for b in range(RAW):
                                with sp.If(n > first + i + (b - PEEL - 1)):
                                    j, r = first + i + b, (PEEL + b) % RAW
                                    sp.wait_ge(gu_lo_ok, j - (RAW - 1))
                                    sp.wait_ge(dn_lo_ok, j - (RAW - 1))
                                    e = sp.value_load(ctl[0:1, bass.ds(j - PEEL, 1)], min_val=0, max_val=E - 1)
                                    load_weights(e, r)
                                    sp.wait_ge(hm_ok, j - (RAW - 1))
                                    load_row(e, r)
                            sp.nop()
            for m in range(KD):
                sp.wait_ge(out_ok, m + 1)
                sp.dma_start(out_d[m], o_sb[:, m, :]).then_inc(stored, 16)
            sp.wait_ge(stored, 16 * KD)

        @block.tensor
        def _(pe):
            def keep_warm(count, bank):
                for _ in range(count):
                    pe.matmul(banks[bank], warm[:, 0:P], warm[:, :], start=True, stop=True)

            pe.wait_ge(warm_ok, 1)
            keep_warm(6, 7)
            pe.wait_ge(b_hi_ok, 1)
            pe.wait_ge(one_ok, 2)
            for t in range(NT):
                pe.matmul(banks[t][:, 0:D], one_r[:, :], b_hi[:, :], start=True, stop=False)
            pe.wait_ge(b_lo_ok, 1)
            for t in range(NT):
                pe.matmul(banks[t][:, 0:D], one_r[:, :], b_lo[:, :], start=False, stop=False)
            keep_warm(1, 7)
            for c in range(KP):
                pe.wait_ge(tok_hi_ok, 2 * c + 2)
                for p in range(3):
                    if p == 1:
                        pe.wait_ge(tok_lo_ok, 2 * c + 1)
                    if p == 2:
                        pe.wait_ge(tok_lo_ok, 2 * c + 2)
                    for t in range(NT):
                        mm = pe.matmul(banks[t][:, 0:D], (xp_hi, xp_lo, xp_hi)[p][:, c, t * P:(t + 1) * P],
                                       (wt_hi, wt_hi, wt_lo)[p][:, c, :], start=False,
                                       stop=(c == KP - 1 and p == 2))
                        if c == KP - 1 and p == 2:
                            mm.then_inc(tok_mm, 1)

            def transpose_tile(nth, t, bank):
                pe.wait_ge(xn_ready, nth * NT + t + 1)
                for k in range(KD):
                    mm = pe.transpose(banks[bank][:, k * P:(k + 1) * P], xn[:, t, k * P:(k + 1) * P], ident)
                mm.then_inc(xt_ps, 1)

            def value_half(t, half):
                pe.wait_ge(xt_hi_ok, t + 1)
                if t >= 2:
                    pe.wait_ge(v_ok_a if half == 0 else v_ok_v, t - 1)
                else:
                    pe.wait_ge(h_ready, v_bank(t, half) + 1)
                cols = slice(half * BANK, (half + 1) * BANK)
                for i in range(3 * KD):
                    p, k = i // KD, i % KD
                    if i == 2 * KD:
                        pe.wait_ge(xt_lo_ok, t + 1)
                    xs = (xt_hi, xt_hi, xt_lo)[p][:, k, t * P:(t + 1) * P]
                    ws = (w_hi3, w_lo3, w_hi3)[p][:, 0, k, cols]
                    mm = pe.matmul(banks[v_bank(t, half)], xs, ws, start=(i == 0), stop=(i == 3 * KD - 1))
                mm.then_inc(v_mm_a if half == 0 else v_mm_v, 1)

            pe.wait_ge(const_in, 16)
            keep_warm(6, 6)
            transpose_tile(0, 0, X1_BANK[0])
            keep_warm(2, 6)
            transpose_tile(0, 1, X1_BANK[1])
            keep_warm(1, 6)
            pe.wait_ge(w_hi_v, 1)
            pe.wait_ge(w_lo_v[0], 1)
            value_half(0, 0)
            value_half(1, 0)
            transpose_tile(0, 2, X1_BANK[2])
            pe.wait_ge(w_hi_v, 2)
            pe.wait_ge(w_lo_v[1], 1)
            value_half(0, 1)
            pe.wait_ge(sel_ok, 1)
            pe.wait_ge(xt_lo_ok, 1)
            pe.matmul(banks[X1_BANK[0]][0:1, 0:EARLY], number, early_col[:, :], start=True,
                      stop=True).then_inc(early_mm, 1)
            value_half(1, 1)
            transpose_tile(0, 3, X1_BANK[3])
            for t in range(2, NT):
                for half in range(2):
                    value_half(t, half)

            def project(g, which, bank, done):
                cols = slice(g * P, (g + 1) * P)
                for i in range(3 * KD):
                    k, p = i // 3, i % 3
                    ws = (w_hi3, w_hi3, w_lo3)[p][:, which, k, cols]
                    xs = (xt_hi, xt_lo, xt_hi)[p][:, k, :]
                    mm = pe.matmul(banks[bank], ws, xs, start=(i == 0), stop=(i == 3 * KD - 1))
                mm.then_inc(done, 1)

            def scores(g):
                pe.wait_ge(q_ok, g + 1)
                pe.wait_ge(k_ok, g + 1)
                if g < 2:
                    pe.wait_ge(v_ok_a, NT)
                    pe.wait_ge(v_ok_v, NT)
                else:
                    pe.wait_ge(sc_out, g - 1)
                for t in range(NT):
                    for a in range(2):
                        rows = slice(HEAD * a, HEAD * (a + 1))
                        mm = pe.matmul(score_ps[g % 2][:, (a * NT + t) * P:(a * NT + t + 1) * P],
                                       q_t[rows, g % 2, t * P:(t + 1) * P],
                                       k_t[rows, g % 2, t * P:(t + 1) * P], start=True, stop=True)
                mm.then_inc(sc_mm, 1)

            def values_of(g, tiles, bank):
                for a in range(2):
                    for t in tiles:
                        mm = pe.matmul(banks[bank][HEAD * a:HEAD * (a + 1), t * P:(t + 1) * P],
                                       v_sb[:, t, (2 * g + a) * HEAD:(2 * g + a + 1) * HEAD],
                                       p_t[:, g % 2, a * NT + t if g < NG - 1 else 2 * t + a, :],
                                       start=True, stop=True)
                mm.then_inc(pv_mm, 1)

            def values(g):
                pe.wait_ge(pt_ok, g + 1)
                if g < 2:
                    pe.wait_ge(xt_lo_ok, NT)
                    pe.wait_ge(early_ok, 1)
                else:
                    pe.wait_ge(o_full_ok, g - 1)
                values_of(g, range(NT), 4 + g % 2)

            def output(g, tiles=range(NT)):
                half = tiles[0] // 2 if g == NG - 1 else 0
                pe.wait_ge(o_hi_ok, g + 1 + half)
                if g < NG - LAST:
                    pe.wait_ge(o_lo_ok, g + 1)
                else:
                    pe.wait_ge(o_lo_last, g - (NG - LAST) + 1 + half)
                pe.wait_ge(wu_hi_ok, g + 1)
                pe.wait_ge(wu_lo_ok, g + 1)
                for t in tiles:
                    for p in range(3):
                        os_ = (o_hi, o_hi, o_lo)[p][:, g, t * P:(t + 1) * P]
                        ws = (wu_hi, wu_lo, wu_hi)[p][:, g, :]
                        mm = pe.matmul(banks[U_BANK[t]][:, 0:D], os_, ws, start=(g == 0 and p == 0),
                                       stop=(g == NG - 1 and p == 2))
                    if g == NG - 1:
                        mm.then_inc(u_mm, 1)

            pe.wait_ge(w_hi_ok, 2)
            pe.wait_ge(w_lo_q, 1)
            pe.wait_ge(w_lo_k, 1)

            def query_key(g):
                if g >= 1:
                    pe.wait_ge(q_ok, g)
                project(g, 1, 6, q_mm)
                if g >= 1:
                    pe.wait_ge(k_ok, g)
                project(g, 2, 7, k_mm)

            query_key(0)
            pe.wait_ge(q_ok, 1)
            project(1, 1, 6, q_mm)
            scores(0)
            pe.wait_ge(k_ok, 1)
            project(1, 2, 7, k_mm)
            for g in range(NG - 2):
                if g >= 1:
                    scores(g)
                query_key(g + 2)
                if g >= 1:
                    values(g - 1)
            scores(NG - 2)
            scores(NG - 1)
            pe.wait_ge(q_ok, NG)
            pe.wait_ge(k_ok, NG)
            for g in range(2):
                output(g, [0, 1])
            values(NG - 3)
            for g in range(2, NG - 3):
                output(g, [0, 1])
            pe.wait_ge(sc_out, NG - 1)
            for g in range(3):
                output(g, [2, 3])
            values(NG - 2)
            for g in range(3, NG - 3):
                output(g, [2, 3])
            output(NG - 3)
            pe.wait_ge(pt_ok, NG)
            pe.wait_ge(o_full_ok, NG - 2)
            values_of(NG - 1, (0, 1), LAST_BANK[0])
            output(NG - 2, [0, 1])
            output(NG - 2, [2])
            output(NG - 1, [0])
            output(NG - 1, [1])
            pe.wait_ge(pt_ok, NG + 1)
            values_of(NG - 1, (2, 3), LAST_BANK[1])
            output(NG - 2, [3])
            keep_warm(1, 3)
            output(NG - 1, [2, 3])
            keep_warm(1, 3)

            def add_residual(t):
                pe.wait_ge(h2_ok, t + 1)
                for k in range(KD):
                    pe.matmul(banks[4 + k][:, t * P:(t + 1) * P], h[:, t, k * P:(k + 1) * P], ident,
                              start=(t == 0), stop=False, skip_group_check=True)

            add_residual(0)
            add_residual(1)
            keep_warm(1, 3)
            add_residual(2)
            transpose_tile(1, 0, X2_BANK[0])
            add_residual(3)
            transpose_tile(1, 1, X2_BANK[1])
            keep_warm(2, 0)
            transpose_tile(1, 2, X2_BANK[2])
            keep_warm(1, 0)
            transpose_tile(1, 3, X2_BANK[3])
            keep_warm(2, 0)

            pe.wait_ge(rt_hi_ok, 1)
            pe.wait_ge(rt_lo_ok, 1)
            pe.wait_ge(xt_hi_ok, 2 * NT)
            for i in range(3 * KD):
                p, k = i // KD, i % KD
                if i == 2 * KD:
                    pe.wait_ge(xt_lo_first, 2)
                    pe.wait_ge(xt_lo_ok, 2 * NT - 2)
                mm = pe.matmul(banks[2], (rt_hi, rt_lo, rt_hi)[p][:, k, :], (xt_hi, xt_hi, xt_lo)[p][:, k, :],
                               start=(i == 0), stop=(i == 3 * KD - 1))
            mm.then_inc(rt_mm, 1)

            def half_item(j, b, half, bank, done):
                for i in range(3 * KD):
                    k, p = i // 3, i % 3
                    at = k * 2 * P + half * P
                    ws = (ex_hi, ex_hi, ex_lo)[p][:, b % 2, at:at + P]
                    xs = (xt_hi, xt_lo, xt_hi)[p][:, k, :]
                    mm = pe.matmul(bank, ws, xs, start=(i == 0), stop=(i == 3 * KD - 1))
                mm.then_inc(done, 1)

            def gate(j, b):
                pe.wait_ge(gu_hi_ok, j + 1)
                pe.wait_ge(gu_lo_ok, j + 1)
                if not (type(j) is int and j < 2):
                    pe.wait_ge(silu_ok, j - 1)
                half_item(j, b, 0, gate_bank(b), gate_mm)

            def up(j, b):
                if not (type(j) is int and j < 2):
                    pe.wait_ge(hm_ok, j - 1)
                half_item(j, b, 1, up_bank(b), up_mm)

            def down(j, b):
                pe.wait_ge(dn_hi_ok, j + 1)
                pe.wait_ge(dn_lo_ok, j + 1)
                pe.wait_ge(hm_hi_ok, j + 1)
                for p in range(3):
                    if p == 2:
                        pe.wait_ge(hm_lo_ok, j + 1)
                    for m in range(KD):
                        ws = (ex_hi, ex_lo, ex_hi)[p][:, b % 2, GU + m * P:GU + (m + 1) * P]
                        hs = (hm_hi, hm_hi, hm_lo)[p][:, b % 2, :]
                        mm = pe.matmul(banks[4 + m], ws, hs, start=False, stop=(p == 2),
                                       skip_group_check=True)
                mm.then_inc(down_mm, 1)

            gate(0, 0)
            pe.wait_ge(lt_ok, 1)
            for t in range(NT):
                mm = pe.transpose(banks[3][:, t * E:(t + 1) * E], logits_t[:, t * P:(t + 1) * P],
                                  consts[0:E, C_IDENT:C_IDENT + E])
            mm.then_inc(lt_mm, 1)
            up(0, 0)
            gate(1, 1)
            up(1, 1)
            pe.wait_ge(chosen_ok, 1)
            for t in range(NT):
                mm = pe.matmul(banks[2][0:E, 0:1], chosen[:, t, :], ones, start=(t == 0), stop=(t == NT - 1))
            mm.then_inc(cnt_mm, 1)
            gate(2, 2)
            pe.wait_ge(act_ok, 1)
            pe.matmul(banks[2][0:E, 1:2], before, active[:, :], start=True, stop=True).then_inc(pos_mm, 1)
            down(0, 0)
            up(2, 2)
            pe.wait_ge(place_ok, 1)
            pe.matmul(banks[2][0:1, 0:LIST], number, place[:, :], start=True, stop=True)
            pe.matmul(banks[2][0:1, CTL_N:CTL_N + 1], active[:, :], ones[0:E, :], start=True,
                      stop=True).then_inc(list_mm, 1)
            pe.wait_ge(comb_ok, 1)
            for t in range(NT):
                mm = pe.transpose(banks[3][0:E, t * P:(t + 1) * P], comb[:, t, :], ident)
            mm.then_inc(ct_mm, 1)
            gate(3, 3)
            down(1, 1)
            pe.wait_ge(ct_ok, 1)
            pe.matmul(banks[3], early_sel[:, 0, :], comb_t[:, :], start=True, stop=True).then_inc(cb_mm, 1)
            up(3, 3)
            pe.wait_ge(ctl_ok, 1)
            pe.matmul(banks[2], early_sel[:, 1, :], comb_t[:, :], start=True, stop=True).then_inc(cb_mm, 1)
            n = pe.value_load(ctl[0:1, CTL_N:CTL_N + 1], min_val=TOP_K - EARLY, max_val=E)
            gate(4, 0)
            down(2, 2)
            up(4, 0)
            down(3, 3)
            gate(5, 1)
            up(5, 1)
            down(4, 0)
            with pe.Fori(PEEL, PEEL + E, SPAN) as first:
                with pe.If(n > first + (-PEEL - 1)):
                    with pe.Fori(0, SPAN, RAW) as i:
                        with pe.If(n > first + i + (-PEEL - 1)):
                            for b in range(RAW):
                                j, r = first + i + b, (PEEL + b) % RAW
                                with pe.If(n > first + i + (b - PEEL)):
                                    gate(j, r)
                                    up(j, r)
                                with pe.If(n > first + i + (b - PEEL - 1)):
                                    down(j - 1, (r - 1) % RAW)
                            pe.nop()

        @block.scalar
        def _(act):
            def split_hi(dst, src, done):
                nc.scalar.activation(dst, src, ACT.Copy).then_inc(done, 1)

            act.wait_ge(bias_in, 16)
            split_hi(b_hi[:, :], b_tok[:, :], b_hi_ok)
            act.wait_ge(one_ok, 1)
            split_hi(one_r[:, :], one_row[:, :], one_ok)
            for c in range(KP):
                act.wait_ge(patches_in[c], 16)
                split_hi(xp_hi[:, c, :], xp3[:, c, :], tok_hi_ok)
                act.wait_ge(w_tok_in[c], 16)
                split_hi(wt_hi[:, c, :], w_tok[:, c, :], tok_hi_ok)

            def root_table():
                nc.scalar.activation(std[:, NT:NT + 1], eps_col, ACT.Sqrt)

            act.wait_ge(eps_ok, 1)
            root_table()

            def root(nth, t):
                act.wait_ge(var_ok, nth * NT + t + 1)
                nc.scalar.activation(std[:, t:t + 1], mv[:, t, 1:2], ACT.Sqrt, bias=eps_col).then_inc(std_ok, 1)

            def xt_high(nth, t, bank):
                act.wait_ge(xt_ps, nth * NT + t + 1)
                src = banks[bank][:, 0:D].rearrange("p (k n) -> p k n", k=KD)
                if nth == 1 and t < 2:
                    nc.scalar.activation(xt_full[:, t], src, ACT.Copy).then_inc(xt_full_ok, 1)
                split_hi(xt_hi[:, :, t * P:(t + 1) * P], src, xt_hi_ok)

            def h_copy(t):
                act.wait_ge(xn_ready, t + 1)
                nc.scalar.activation(h[:, t, :], banks[t][:, 0:D], ACT.Copy).then_inc(h_ready, 1)

            def wv_high(half):
                act.wait_ge(w_in[0], 16)
                cols = slice(half * BANK, (half + 1) * BANK)
                split_hi(w_hi3[:, 0, :, cols], stage3[:, 0, :, cols], w_hi_v)

            wv_high(0)
            wv_high(1)
            root(0, 0)
            root(0, 1)
            h_copy(0)
            xt_high(0, 0, X1_BANK[0])
            root(0, 2)
            h_copy(1)
            xt_high(0, 1, X1_BANK[1])
            root(0, 3)
            h_copy(2)
            xt_high(0, 2, X1_BANK[2])
            h_copy(3)

            def v_copy(t):
                act.wait_ge(v_mm_a, t + 1)
                nc.scalar.activation(v_sb[:, t, 0:BANK], banks[v_bank(t, 0)], ACT.Copy).then_inc(v_ok_a, 1)

            v_copy(0)
            act.wait_ge(w_in[1], 16)
            split_hi(w_hi3[:, 1], stage3[:, 1], w_hi_ok)
            act.wait_ge(w_in[2], 16)
            split_hi(w_hi3[:, 2], stage3[:, 2], w_hi_ok)
            xt_high(0, 3, X1_BANK[3])
            for t in range(1, NT):
                v_copy(t)
            nc.scalar.activation(std[:, NT:NT + 1], eps_col, ACT.Exp)
            act.wait_ge(small_in, 32)
            act.wait_ge(rt_zero, 1)
            split_hi(rt_hi[:, :, 0:E], rt_raw[:, :, :], rt_hi_ok)

            def o_high(g):
                act.wait_ge(pv_mm, g + 1)
                if g < NG - LAST:
                    if g >= 2:
                        act.wait_ge(o_lo_ok, g - 1)
                    nc.scalar.activation(o_full[:, g % 2, :], banks[4 + g % 2], ACT.Copy).then_inc(o_full_ok, 1)
                    act.wait_ge(o_full_ok, g + 1)
                    split_hi(o_hi[:, g, :], o_full[:, g % 2, :], o_hi_ok)
                else:
                    split_hi(o_hi[:, g, :], banks[4 + g % 2], o_hi_ok)

            def o_high_half(half):
                act.wait_ge(pv_mm, NG + half)
                cols = slice(half * T // 2, (half + 1) * T // 2)
                split_hi(o_hi[:, NG - 1, cols], banks[LAST_BANK[half]][:, cols], o_hi_ok)

            def gate_up_high(j, b):
                act.wait_ge(raw_in[b], 4 * (j - b) + 16)
                if not (type(j) is int and j < 2):
                    act.wait_ge(up_mm, j - 1)
                split_hi(ex_hi[:, b % 2, 0:GU], raw[:, b, 0:GU], gu_hi_ok)

            def down_high(j, b):
                if not (type(j) is int and j < 2):
                    act.wait_ge(down_mm, j - 1)
                split_hi(ex_hi[:, b % 2, GU:ITEM], raw[:, b, GU:ITEM], dn_hi_ok)

            def silu(j, b):
                act.wait_ge(gate_mm, j + 1)
                if not (type(j) is int and j < 2):
                    act.wait_ge(hm_ok, j - 1)
                nc.scalar.activation(gate_act[:, b % 2, :], gate_bank(b), ACT.Silu).then_inc(silu_ok, 1)

            def h_high(j, b):
                act.wait_ge(hm_ok, j + 1)
                if not (type(j) is int and j < 2):
                    act.wait_ge(down_mm, j - 1)
                split_hi(hm_hi[:, b % 2, :], h_mid[:, b % 2, :], hm_hi_ok)

            def query_key(g):
                if g >= 2:
                    act.wait_ge(sc_mm, g - 1)
                act.wait_ge(q_mm, g + 1)
                nc.scalar.activation(q_t[:, g % 2, :], banks[6], ACT.Copy).then_inc(q_ok, 1)
                act.wait_ge(k_mm, g + 1)
                nc.scalar.activation(k_t[:, g % 2, :], banks[7], ACT.Copy).then_inc(k_ok, 1)

            query_key(0)
            query_key(1)
            act.wait_ge(wu_in, 16)
            for g in range(NG):
                if 1 <= g < NG - 2:
                    query_key(g + 2)
                split_hi(wu_hi[:, g, :], wu_raw[:, g, :], wu_hi_ok)
                if g == NG - 1:
                    o_high(g - 1)
                for half in (range(2) if g == NG - 1 else (None,)):
                    part = slice(0, A8) if half is None else slice(half * HALF, (half + 1) * HALF)
                    act.wait_ge(sc_sub, g + 1 + (half or 0))
                    nc.scalar.activation(pr[:, g % 2, part], sc[:, part, :], ACT.Exp).then_inc(pr_ok, 1)
                if g == 0:
                    query_key(2)
                if 1 <= g < NG - 1:
                    o_high(g - 1)
            root_table()
            act.wait_ge(v_mm_a, NT)
            act.wait_ge(v_mm_v, NT)
            o_high_half(0)
            gate_up_high(0, 0)
            down_high(0, 0)
            o_high_half(1)
            gate_up_high(1, 1)
            down_high(1, 1)

            root(1, 0)
            root(1, 1)
            root(1, 2)
            xt_high(1, 0, X2_BANK[0])
            root(1, 3)
            for t in range(1, NT):
                xt_high(1, t, X2_BANK[t])
            act.wait_ge(rt_mm, 1)
            nc.scalar.activation(logits_t[:, :], banks[2][0:E, :], ACT.Copy).then_inc(lt_ok, 1)
            act.wait_ge(rt_sub, 1)
            nc.scalar.activation(re_[:, :, :], rl[:, :, :], ACT.Exp).then_inc(rt_exp, 1)
            gate_up_high(2, 2)
            silu(0, 0)
            h_high(0, 0)
            gate_up_high(3, 3)
            silu(1, 1)
            down_high(2, 2)
            h_high(1, 1)
            gate_up_high(4, 0)
            silu(2, 2)
            silu(3, 3)
            down_high(3, 3)
            h_high(2, 2)
            gate_up_high(5, 1)
            h_high(3, 3)
            down_high(4, 0)
            silu(4, 0)
            h_high(4, 0)
            down_high(5, 1)
            act.wait_ge(ctl_ok, 1)
            n = act.value_load(ctl[0:1, CTL_N:CTL_N + 1], min_val=TOP_K - EARLY, max_val=E)
            with act.Fori(PEEL, PEEL + E, SPAN) as first:
                with act.If(n > first + (-PEEL - 1)):
                    with act.Fori(0, SPAN, RAW) as i:
                        with act.If(n > first + i + (-PEEL - 1)):
                            for b in range(RAW):
                                with act.If(n > first + i + (b - PEEL - 1)):
                                    j, r = first + i + b, (PEEL + b) % RAW
                                    gate_up_high(j, r)
                                    silu(j - 1, (r - 1) % RAW)
                                    h_high(j - 1, (r - 1) % RAW)
                                    down_high(j, r)
                            act.nop()
            act.wait_ge(down_mm, n + PEEL)
            for m in range(KD):
                nc.scalar.activation(o_sb[:, m, :], banks[4 + m], ACT.Copy).then_inc(out_ok, 1)

        @block.gpsimd
        def _(pool):
            pool.memset(p_t[:, :, :, :], 0.0).then_inc(pt_zero, 1)

            def split_lo(dst, src, hi, done):
                pool.tensor_tensor(dst, src, hi.bitcast(F32), ALU.subtract).then_inc(done, 1)

            for w in (rt_hi, rt_lo):
                ins = pool.memset(w[:, :, :].bitcast(F32), 0.0)
            ins.then_inc(rt_zero, 1)
            pool.wait_ge(w_hi_v, 2)
            second = slice(BANK, 2 * BANK)
            split_lo(w_lo3[:, 0, :, second], stage3[:, 0, :, second], w_hi3[:, 0, :, second], w_lo_v[1])
            pool.wait_ge(w_hi_ok, 1)
            split_lo(w_lo3[:, 1], stage3[:, 1], w_hi3[:, 1], w_lo_q)
            pool.wait_ge(rt_hi_ok, 1)
            split_lo(rt_lo[:, :, 0:E], rt_raw[:, :, :], rt_hi[:, :, 0:E], rt_lo_ok)
            pool.wait_ge(small_in, 32)
            for t in range(NT):
                pool.wait_ge(h_ready, t + 1)
                pool.tensor_tensor(h[:, t, :], h[:, t, :], b_u[:, :], ALU.add).then_inc(hb_ok, 1)
            for g in range(NG):
                pool.wait_ge(wu_hi_ok, g + 1)
                split_lo(wu_lo[:, g, :], wu_raw[:, g, :], wu_hi[:, g, :], wu_lo_ok)
                if 1 <= g <= NG - LAST:
                    pool.wait_ge(o_hi_ok, g)
                    split_lo(o_lo[:, g - 1, :], o_full[:, (g - 1) % 2, :], o_hi[:, g - 1, :], o_lo_ok)
            for r in range(2):
                pool.wait_ge(xt_hi_ok, NT + r + 1)
                pool.wait_ge(xt_full_ok, r + 1)
                cols = slice(r * P, (r + 1) * P)
                split_lo(xt_lo[:, :, cols], xt_full[:, r], xt_hi[:, :, cols], xt_lo_first)

            def gate_up_low(j, b):
                pool.wait_ge(gu_hi_ok, j + 1)
                split_lo(ex_lo[:, b % 2, 0:GU], raw[:, b, 0:GU], ex_hi[:, b % 2, 0:GU], gu_lo_ok)

            def down_low(j, b):
                pool.wait_ge(dn_hi_ok, j + 1)
                split_lo(ex_lo[:, b % 2, GU:ITEM], raw[:, b, GU:ITEM], ex_hi[:, b % 2, GU:ITEM], dn_lo_ok)

            gate_up_low(0, 0)
            for j in range(1, PEEL):
                if j < 3:
                    down_low(j - 1, (j - 1) % RAW)
                    gate_up_low(j, j % RAW)
                else:
                    gate_up_low(j, j % RAW)
                    down_low(j - 1, (j - 1) % RAW)
            down_low(PEEL - 1, (PEEL - 1) % RAW)
            pool.wait_ge(ctl_ok, 1)
            n = pool.value_load(ctl[0:1, CTL_N:CTL_N + 1], min_val=TOP_K - EARLY, max_val=E)
            with pool.Fori(PEEL, PEEL + E, SPAN) as first:
                with pool.If(n > first + (-PEEL)):
                    with pool.Fori(0, SPAN, RAW) as i:
                        with pool.If(n > first + i + (-PEEL)):
                            for b in range(RAW):
                                with pool.If(n > first + i + (b - PEEL)):
                                    gate_up_low(first + i + b, (PEEL + b) % RAW)
                                    down_low(first + i + b, (PEEL + b) % RAW)
                            pool.nop()

        @block.vector
        def _(dve):
            steps = [0]

            def done(ins):
                steps[0] += 1
                ins.then_inc(step, 1)
                return steps[0]

            def need(result):
                dve.wait_ge(step, result)

            def settle():
                dve.wait_ge(step, steps[0])

            def tt(out, a, b, op):
                return dve.tensor_tensor(out, a, b, op)

            dve.memset(warm[:, :], 0.0).then_inc(warm_ok, 1)
            dve.memset(one_row[:, :], 1.0).then_inc(one_ok, 1)
            dve.memset(eps_col, LN_EPS).then_inc(eps_ok, 1)
            done(dve.memset(corr[:, :, E:], OUTDONE))
            dve.wait_ge(b_hi_ok, 1)
            tt(b_lo[:, :], b_tok[:, :], b_hi[:, :].bitcast(F32), ALU.subtract).then_inc(b_lo_ok, 1)
            for c in range(KP):
                dve.wait_ge(tok_hi_ok, 2 * c + 1)
                tt(xp_lo[:, c, :], xp3[:, c, :], xp_hi[:, c, :].bitcast(F32), ALU.subtract).then_inc(tok_lo_ok, 1)
                dve.wait_ge(tok_hi_ok, 2 * c + 2)
                tt(wt_lo[:, c, :], w_tok[:, c, :], wt_hi[:, c, :].bitcast(F32), ALU.subtract).then_inc(tok_lo_ok, 1)
            dve.wait_ge(w_hi_v, 1)
            first = slice(0, BANK)
            tt(w_lo3[:, 0, :, first], stage3[:, 0, :, first], w_hi3[:, 0, :, first].bitcast(F32),
               ALU.subtract).then_inc(w_lo_v[0], 1)

            def summary(nth, t):
                need(stat[nth, t])
                dve.bn_aggr(mv[:, t, :], stats[:, t, :]).then_inc(var_ok, 1)

            def invert(nth, t):
                dve.wait_ge(std_ok, nth * NT + t + 1)
                inverse[nth, t] = done(dve.reciprocal(rstd[:, t:t + 1], std[:, t:t + 1]))

            def normalise(nth, t, src):
                need(inverse[nth, t])
                dve.tensor_scalar(xn[:, t, :], src, mv[:, t, 0:1], rstd[:, t:t + 1],
                                  ALU.subtract, ALU.mult).then_inc(xn_ready, 1)

            stat, inverse = {}, {}

            def xt_low(nth, t, bank):
                dve.wait_ge(xt_hi_ok, nth * NT + t + 1)
                cols = slice(t * P, (t + 1) * P)
                src = banks[bank][:, 0:D].rearrange("p (k n) -> p k n", k=KD)
                tt(xt_lo[:, :, cols], src, xt_hi[:, :, cols].bitcast(F32), ALU.subtract).then_inc(xt_lo_ok, 1)

            def first_norm(t, part):
                src = banks[t][:, 0:D]
                if part == 0:
                    dve.wait_ge(tok_mm, t + 1)
                    stat[0, t] = done(dve.bn_stats(stats[:, t, :], src))
                elif part == 1:
                    summary(0, t)
                elif part == 2:
                    invert(0, t)
                elif part == 3:
                    normalise(0, t, src)
                else:
                    xt_low(0, t, X1_BANK[t])

            for t, part in ((0, 0), (0, 1), (1, 0), (0, 2), (1, 1), (0, 3), (2, 0), (1, 2), (2, 1), (1, 3),
                            (0, 4), (3, 0), (2, 2), (2, 3), (3, 1), (1, 4), (3, 2), (3, 3)):
                first_norm(t, part)
            dve.wait_ge(const_in, 16)
            dve.wait_ge(ebias_in, 32)
            done(dve.scalar_tensor_tensor(out=tied[:, :], in0=e_bias[0:E, :], scalar=bias_col[:, :], in1=before,
                                          op0=ALU.is_equal, op1=ALU.mult))
            settle()
            done(dve.scalar_tensor_tensor(out=ahead[:, :], in0=e_bias[0:E, :], scalar=bias_col[:, :],
                                          in1=tied[:, :], op0=ALU.is_gt, op1=ALU.add))
            settle()
            done(dve.tensor_reduce(rank[:, :], ahead[:, :], AX_X, ALU.add))
            settle()
            done(dve.tensor_scalar(late[:, :], rank[:, :], float(EARLY), None, ALU.is_ge))
            done(dve.tensor_scalar(early_sel[:, :, :], slots[:, 0:SPREAD].unsqueeze(2).broadcast_to([E, SPREAD, P]),
                                   rank[:, :], None, ALU.is_equal))
            dve.tensor_scalar(early_col[:, :], slots[:, 0:EARLY], rank[:, :], None, ALU.is_equal
                              ).then_inc(sel_ok, 1)

            def v_copy(t):
                dve.wait_ge(v_mm_v, t + 1)
                dve.tensor_copy(v_sb[:, t, BANK:2 * BANK], banks[v_bank(t, 1)]).then_inc(v_ok_v, 1)

            xt_low(0, 2, X1_BANK[2])
            v_copy(0)
            dve.wait_ge(early_mm, 1)
            dve.tensor_copy(early_num[:, :], banks[X1_BANK[0]][0:1, 0:EARLY]).then_inc(early_ok, 1)
            xt_low(0, 3, X1_BANK[3])
            v_copy(1)
            dve.wait_ge(w_hi_ok, 2)
            tt(w_lo3[:, 2], stage3[:, 2], w_hi3[:, 2].bitcast(F32), ALU.subtract).then_inc(w_lo_k, 1)
            for t in range(2, NT):
                v_copy(t)

            def o_low(g):
                dve.wait_ge(o_hi_ok, g + 1)
                tt(o_lo[:, g, :], banks[4 + g % 2], o_hi[:, g, :].bitcast(F32), ALU.subtract).then_inc(o_lo_last, 1)

            def o_low_half(half):
                dve.wait_ge(o_hi_ok, NG + half)
                cols = slice(half * T // 2, (half + 1) * T // 2)
                tt(o_lo[:, NG - 1, cols], banks[LAST_BANK[half]][:, cols], o_hi[:, NG - 1, cols].bitcast(F32),
                   ALU.subtract).then_inc(o_lo_last, 1)

            def over_keys(x, part):
                return x[:, part].unsqueeze(2).broadcast_to([P, part.stop - part.start, BLOCK])

            def less_max(part):
                tt(sc[:, part, :], sc[:, part, :], over_keys(mx, part), ALU.subtract).then_inc(sc_sub, 1)

            def normalised(g, part, nth, between=None):
                dve.wait_ge(pr_ok, nth)
                done(dve.tensor_reduce(sm[:, part], pr[:, g % 2, part], AX_X, ALU.add))
                settle()
                done(dve.reciprocal(ri[:, part], sm[:, part]))
                settle()
                done(tt(pn[:, part, :], pr[:, g % 2, part], over_keys(ri, part), ALU.mult))
                if between:
                    between()
                settle()
                if g >= 2:
                    dve.wait_ge(pv_mm, g - 1)
                for r in range(P // BLOCK):
                    rows = slice(r * BLOCK, (r + 1) * BLOCK)
                    ins = dve.transpose(p_t[rows, g % 2, part, rows], pn[rows, part])
                ins.then_inc(pt_ok, 1)

            dve.wait_ge(const_in, 16)
            dve.wait_ge(pt_zero, 1)
            for g in range(NG):
                dve.wait_ge(sc_mm, g + 1)
                if g >= 1:
                    dve.wait_ge(pr_ok, g)
                src = score_ps[g % 2][:, :].rearrange("p (a n) -> p a n", a=A8)
                by_tile = sc[:, :, :].rearrange("p (t a) c -> p a t c", a=2)
                for r in range(P // BLOCK):
                    part = slice(r * BLOCK, (r + 1) * BLOCK)
                    if g < NG - 1:
                        parts = [(sc[part], src[part, :, part], mask8[part])]
                    else:
                        parts = [(by_tile[part, a], src[part, a * NT:(a + 1) * NT, part], mask8[part, 0:NT])
                                 for a in range(2)]
                    for dst, block, masks in parts:
                        ins = dve.scalar_tensor_tensor(out=dst, in0=block, scalar=SCORE_SCALE, in1=masks,
                                                       op0=ALU.mult, op1=ALU.add)
                ins.then_inc(sc_out, 1)
                settle()
                dve.wait_ge(sc_out, g + 1)
                done(dve.tensor_reduce(mx[:, :], sc[:, :, :], AX_X, ALU.max))
                settle()
                if g < NG - 1:
                    less_max(slice(0, A8))
                    normalised(g, slice(0, A8), g + 1)
                else:
                    less_max(slice(0, HALF))
                    less_max(slice(HALF, A8))
                    o_low(g - 1)
                    normalised(g, slice(0, HALF), g + 1)
                    normalised(g, slice(HALF, A8), g + 2, lambda: o_low_half(0))
            def second_norm(t, part):
                src = h[:, t, :]
                if part == 0:
                    dve.wait_ge(u_mm, t + 1)
                    dve.wait_ge(hb_ok, t + 1)
                    tt(src, banks[U_BANK[t]][:, 0:D], src, ALU.add).then_inc(h2_ok, 1)
                elif part == 1:
                    dve.wait_ge(h2_ok, t + 1)
                    stat[1, t] = done(dve.bn_stats(stats[:, t, :], src))
                elif part == 2:
                    summary(1, t)
                elif part == 3:
                    invert(1, t)
                elif part == 4:
                    normalise(1, t, src)
                else:
                    xt_low(1, t, X2_BANK[t])

            for t, part in ((0, 0), (0, 1), (1, 0)):
                second_norm(t, part)
            o_low_half(1)
            for t, part in ((0, 2), (1, 1), (0, 3), (1, 2), (2, 0), (0, 4), (1, 3), (2, 1), (1, 4), (3, 0),
                            (2, 2), (3, 1), (2, 3), (3, 2), (2, 4), (3, 3), (3, 4), (2, 5), (3, 5)):
                second_norm(t, part)

            def h_make(j, b, row=None):
                dve.wait_ge(silu_ok, j + 1)
                act_g = gate_act[:, b % 2, :]
                if row is not None:
                    tt(act_g, act_g, row, ALU.mult).then_inc(gc_ok, 1)
                    dve.wait_ge(gc_ok, j - SHARED + 1)
                dve.wait_ge(up_mm, j + 1)
                if not (type(j) is int and j < 2):
                    dve.wait_ge(hm_hi_ok, j - 1)
                    dve.wait_ge(hm_lo_ok, j - 1)
                tt(h_mid[:, b % 2, :], up_bank(b), act_g, ALU.mult).then_inc(hm_ok, 1)

            def h_low(j, b):
                if not (type(j) is int and j < 2):
                    dve.wait_ge(down_mm, j - 1)
                dve.wait_ge(hm_hi_ok, j + 1)
                tt(hm_lo[:, b % 2, :], h_mid[:, b % 2, :], hm_hi[:, b % 2, :].bitcast(F32),
                   ALU.subtract).then_inc(hm_lo_ok, 1)

            def over_experts(x):
                return x.unsqueeze(2).broadcast_to([P, NT, E])

            dve.wait_ge(lt_mm, 1)
            logits = banks[3][:, 0:NT * E].rearrange("p (t e) -> p t e", t=NT)
            done(dve.tensor_reduce(r4[:, 0, :], logits, AX_X, ALU.max))
            settle()
            tt(rl[:, :, :], logits, over_experts(r4[:, 0, :]), ALU.subtract).then_inc(rt_sub, 1)
            dve.wait_ge(rt_exp, 1)
            done(dve.tensor_reduce(r4[:, 1, :], re_[:, :, :], AX_X, ALU.add))
            settle()
            done(dve.reciprocal(r4[:, 2, :], r4[:, 1, :]))
            settle()
            done(tt(rw[:, :, :], re_[:, :, :], over_experts(r4[:, 2, :]), ALU.mult))
            settle()
            done(tt(corr[:, :, 0:E], rw[:, :, :], e_bias[:, :].unsqueeze(1).broadcast_to([P, NT, E]), ALU.add))
            settle()
            for t in range(NT):
                done(dve.max(top8[:, t, :], corr[:, t, :]))
            settle()
            for t in range(NT):
                done(dve.match_replace(rest[:, t, :], top8[:, t, :], corr[:, t, :], MASKED))
            settle()
            dve.tensor_scalar(chosen[:, :, :], rest[:, :, 0:E], MASKED, None, ALU.is_equal).then_inc(chosen_ok, 1)
            h_make(0, 0)
            dve.wait_ge(chosen_ok, 1)
            done(tt(picked[:, :, :], rw[:, :, :], chosen[:, :, :], ALU.mult))
            dve.wait_ge(cnt_mm, 1)
            dve.tensor_scalar(active[:, :], banks[2][0:E, 0:1], 1.0, late[:, :], ALU.min, ALU.mult).then_inc(act_ok, 1)
            settle()
            done(dve.tensor_reduce(r4[:, 3, :], picked[:, :, :], AX_X, ALU.add))
            h_low(0, 0)
            settle()
            done(dve.tensor_scalar(r4[:, 4, :], r4[:, 3, :], NORM_MIN, None, ALU.max))
            settle()
            done(dve.reciprocal(r4[:, 5, :], r4[:, 4, :]))
            dve.wait_ge(pos_mm, 1)
            done(dve.tensor_copy(pos[:, :], banks[2][0:E, 1:2]))
            settle()
            tt(comb[:, :, :], picked[:, :, :], over_experts(r4[:, 5, :]), ALU.mult).then_inc(comb_ok, 1)
            dve.wait_ge(act_ok, 1)
            dve.tensor_scalar(place[:, :], slots, pos[:, :], active[:, :], ALU.is_equal,
                              ALU.mult).then_inc(place_ok, 1)
            h_make(1, 1)
            dve.wait_ge(list_mm, 1)
            dve.tensor_copy(ctl[:, :], banks[2][0:1, 0:CTL_N + 1]).then_inc(ctl_ok, 1)
            dve.wait_ge(ct_mm, 1)
            dve.tensor_copy(comb_t[:, :], banks[3][0:E, :]).then_inc(ct_ok, 1)
            h_low(1, 1)
            dve.wait_ge(ctl_ok, 1)
            dve.wait_ge(cb_mm, 1)
            h_make(2, 2, banks[3])
            h_low(2, 2)
            n = dve.value_load(ctl[0:1, CTL_N:CTL_N + 1], min_val=TOP_K - EARLY, max_val=E)
            dve.wait_ge(cb_mm, 2)
            h_make(3, 3, banks[2])
            h_low(3, 3)
            for j in range(RAW, PEEL):
                dve.wait_ge(cb_in[j % RAW], 16)
                h_make(j, j % RAW, comb_bc[:, j % RAW, :])
                h_low(j, j % RAW)
            with dve.Fori(PEEL, PEEL + E, SPAN) as first:
                with dve.If(n > first + (-PEEL)):
                    with dve.Fori(0, SPAN, RAW) as i:
                        with dve.If(n > first + i + (-PEEL)):
                            for b in range(RAW):
                                with dve.If(n > first + i + (b - PEEL)):
                                    j, r = first + i + b, (PEEL + b) % RAW
                                    dve.wait_ge(cb_in[r], 4 * (j - r))
                                    h_make(j, r, comb_bc[:, r, :])
                                    h_low(j, r)
                            dve.nop()


def _constants():
    import numpy as np
    c = np.zeros((P, C_COLS), np.float32)
    c[:, C_IDENT:C_IDENT + P] = np.eye(P, dtype=np.float32)
    row = np.arange(P)[:, None] % BLOCK
    col = np.arange(BLOCK)[None, :]
    seen = (row // SEQ == col // SEQ) & (col <= row)
    c[:, C_MASK:C_MASK + MASK_COPIES * BLOCK] = np.tile(np.where(seen, 0.0, MASKED), (1, MASK_COPIES))
    c[0:32, C_BEFORE:C_BEFORE + 32] = np.triu(np.ones((32, 32)), 1)
    c[0:32, C_SLOT:C_SLOT + LIST] = np.arange(LIST)[None]
    c[0:32, C_NUMBER] = np.arange(32)
    c[:, C_ONE] = 1.0
    return c


def kernel(x, L0_tok_W, L0_tok_b, L0_attn_w_q, L0_attn_w_k, L0_attn_w_v, L0_attn_w_u, L0_attn_b_u,
           L0_ffn_router_weight, L0_ffn_e_score_bias, L0_ffn_gate_up_proj, L0_ffn_down_proj,
           L0_ffn_shared_gate_w, L0_ffn_shared_up_w, L0_ffn_shared_down_w):
    import numpy as np
    import concourse.bacc as bacc
    from concourse.bass_utils import run_bass_kernel_spmd

    def rows(a):
        a = np.asarray(a)
        return np.ascontiguousarray(a.reshape(a.shape[0] // P, P, a.shape[1]))

    x = np.asarray(x)
    nb, ch, height, width = x.shape
    side = 16
    patches = x.reshape(nb, ch, height // side, side, width // side, side).transpose(0, 2, 3, 1, 4, 5)
    patches = patches.reshape(-1, ch * side * side)
    d = L0_tok_W.shape[0]

    def item(gate_up, down):
        n = gate_up.shape[0]
        gu = gate_up.transpose(0, 2, 1).reshape(n, d // P, P, 2 * P).transpose(0, 2, 1, 3).reshape(n, P, -1)
        return np.concatenate([gu, down.transpose(0, 2, 1)], axis=2)

    sg, su, sd = (np.asarray(a) for a in (L0_ffn_shared_gate_w, L0_ffn_shared_up_w, L0_ffn_shared_down_w))
    halves = sg.shape[0] // P
    shared_gu = np.concatenate([sg.reshape(halves, P, d), su.reshape(halves, P, d)], axis=1)
    shared_dn = sd.reshape(d, halves, P).transpose(1, 0, 2)
    experts = np.concatenate([item(np.asarray(L0_ffn_gate_up_proj), np.asarray(L0_ffn_down_proj)),
                              item(shared_gu, shared_dn)], axis=0)
    arrays = {
        "patches_t": rows(patches.T),
        "w_tok_t": rows(np.asarray(L0_tok_W).T),
        "b_tok_row": np.asarray(L0_tok_b)[None],
        "w_q": rows(L0_attn_w_q),
        "w_k": rows(L0_attn_w_k),
        "w_v": rows(L0_attn_w_v),
        "w_u": rows(L0_attn_w_u),
        "b_u_row": np.asarray(L0_attn_b_u)[None],
        "router_t": rows(np.asarray(L0_ffn_router_weight).T),
        "expert_bias_row": np.asarray(L0_ffn_e_score_bias)[None],
        "expert_weights": np.ascontiguousarray(experts),
        "constants": _constants(),
    }
    nc = bacc.Bacc("TRN2", target_bir_lowering=False, num_devices=1)
    args = [nc.dram_tensor(k, a.shape, F32, kind="ExternalInput").ap() for k, a in arrays.items()]
    out = nc.dram_tensor("out_t", (d // P, P, patches.shape[0]), F32, kind="ExternalOutput").ap()
    vit_block(nc, *args, out)
    r = run_bass_kernel_spmd(nc, [arrays], core_ids=[0])
    out_t = r.results[0]["out_t"]
    return np.ascontiguousarray(out_t.reshape(d, -1).T).reshape(nb, -1, d)
```
